# Optimizing a Trainium2 kernel written in Bass

```python
import numpy as np
import jax
import jax.numpy as jnp

def _softmax(x, axis=-1):
    return jax.nn.softmax(x, axis=axis)

def _gelu(x):
    return jax.nn.gelu(x, approximate=True)

def _silu(x):
    return jax.nn.silu(x)

def _sigmoid(x):
    return jax.nn.sigmoid(x)

def _layernorm(x, axis=-1, eps=1e-05):
    m = jnp.mean(x, axis=axis, keepdims=True)
    v = jnp.var(x, axis=axis, keepdims=True)
    return (x - m) / jnp.sqrt(v + eps)

def _scatter_add(tgt, idx, src, axis=0):
    return tgt.at[idx].add(src)

def _segment_sum(src, seg, n):
    return jax.ops.segment_sum(src, seg, n)
kernel_name = 'mk_vit_tower_postln_d1_tok_img256_r4_409163'

def setup_inputs(seed: int=0):
    np.random.seed(seed)
    _w = jnp.asarray

    def _rec_inputs():
        import jax
        import jax.numpy as jnp
        _rk = jax.random.key(seed)
        x = -7.10856e-05 + 0.999911 * jax.random.normal(jax.random.fold_in(_rk, 1), (8, 64, 128, 64), jnp.float32)
        return x
    x = _rec_inputs()

    def _L0_tok_setup():
        import jax, jax.numpy as jnp
        import numpy as np
        PATCH_LEN = 16
        STRIDE = 8
        PAD = 8
        key = jax.random.key(seed)
        k1, k2 = jax.random.split(key)
        x = jax.random.normal(k1, (32, 64, 128, 64), dtype=jnp.float32)
        in_feat = 64 * (PATCH_LEN // 2 + 1) * 2
        W = jax.random.normal(k2, (64, in_feat), dtype=jnp.float32) * 0.02
        return {'x': x, 'W': W}
    _L0_tok_all = _L0_tok_setup()
    _L0_tok_in = {k: v for k, v in _L0_tok_all.items() if k in ('W',)}
    del _L0_tok_all

    def _L0_attn_setup():
        import jax, jax.numpy as jnp
        import numpy as np
        TEMPERATURE = 1.0
        W_BLEND = 0.8
        EPS = 1e-12

        def _l2norm(x):
            n = jnp.sqrt(jnp.sum(x * x, axis=-1, keepdims=True))
            return x / jnp.maximum(n, EPS)
        key = jax.random.key(seed)
        feats = jax.random.normal(key, (4, 512, 64), dtype=jnp.float32)
        return {'feats': feats}
    _L0_attn_all = _L0_attn_setup()
    _L0_attn_in = {k: v for k, v in _L0_attn_all.items() if k in ()}
    del _L0_attn_all

    def _L0_ffn_setup():
        import jax, jax.numpy as jnp
        import numpy as np
        NUM_EXPERTS = 8
        TOP_K = 2
        B, S, D = (8, 2048, 64)

        def _moe(tokens, router_w, w1, b1, w2, b2):
            N = tokens.shape[0]
            E = router_w.shape[0]
            logits = tokens.astype(jnp.float32) @ router_w.astype(jnp.float32).T
            probs = jax.nn.softmax(logits, axis=-1)
            rw, re = jax.lax.top_k(probs, TOP_K)
            if TOP_K > 1:
                rw = rw / jnp.maximum(rw.sum(-1, keepdims=True), 1e-12)
            rw = rw.astype(tokens.dtype)
            combine = jnp.zeros((N, E), tokens.dtype).at[jnp.arange(N)[:, None], re].set(rw)
            out = tokens
            for e in range(E):
                h = jax.nn.gelu(tokens @ w1[e] + b1[e], approximate=False)
                y = h @ w2[e] + b2[e]
                out = out + combine[:, e:e + 1] * y
            return out
        key = jax.random.key(seed)
        ks = jax.random.split(key, 4)
        scale = 1.0 / np.sqrt(D).astype(np.float32)
        return {'input_embeddings': jax.random.normal(ks[0], (B, S, D), jnp.float32), 'router_w': jax.random.normal(ks[1], (NUM_EXPERTS, D), jnp.float32) * scale, 'w1': jax.random.normal(ks[2], (NUM_EXPERTS, D, D), jnp.float32) * scale, 'b1': jnp.zeros((NUM_EXPERTS, D), jnp.float32), 'w2': jax.random.normal(ks[3], (NUM_EXPERTS, D, D), jnp.float32) * scale, 'b2': jnp.zeros((NUM_EXPERTS, D), jnp.float32)}
    _L0_ffn_all = _L0_ffn_setup()
    _L0_ffn_in = {k: v for k, v in _L0_ffn_all.items() if k in ('router_w', 'w1', 'b1', 'w2', 'b2')}
    del _L0_ffn_all
    return {'x': x, 'L0_tok_W': _L0_tok_in['W'], 'L0_ffn_router_w': _L0_ffn_in['router_w'], 'L0_ffn_w1': _L0_ffn_in['w1'], 'L0_ffn_b1': _L0_ffn_in['b1'], 'L0_ffn_w2': _L0_ffn_in['w2'], 'L0_ffn_b2': _L0_ffn_in['b2']}

def reference(x, L0_tok_W, L0_ffn_router_w, L0_ffn_w1, L0_ffn_b1, L0_ffn_w2, L0_ffn_b2):
    import jax
    import jax.numpy as jnp

    def _L0_tok_ref(x, W):
        import jax, jax.numpy as jnp
        import numpy as np
        PATCH_LEN = 16
        STRIDE = 8
        PAD = 8
        B, C, T, V = x.shape
        xp = jnp.pad(x, ((0, 0), (0, 0), (0, PAD), (0, 0)), mode='edge')
        Tp = T + PAD
        N = (Tp - PATCH_LEN) // STRIDE + 1
        idx = jnp.arange(N)[:, None] * STRIDE + jnp.arange(PATCH_LEN)[None, :]
        patches = xp[:, :, idx, :]
        patches = jnp.transpose(patches, (0, 4, 2, 3, 1))
        xf = jnp.fft.rfft(patches, axis=-2, norm='ortho')
        F = xf.shape[-2]
        x_real = xf.real.reshape(B, V, N, F * C)
        x_imag = xf.imag.reshape(B, V, N, F * C)
        x_emb = jnp.concatenate([x_real, x_imag], axis=-1)
        x_emb = x_emb @ W.T
        return x_emb.reshape(B, V * N, -1)

    def _L0_attn_ref(feats):
        import jax, jax.numpy as jnp
        import numpy as np
        TEMPERATURE = 1.0
        W_BLEND = 0.8
        EPS = 1e-12

        def _l2norm(x):
            n = jnp.sqrt(jnp.sum(x * x, axis=-1, keepdims=True))
            return x / jnp.maximum(n, EPS)
        B, N, C = feats.shape
        f = _l2norm(feats.reshape(B * N, C))
        scores = jnp.matmul(f, f.T) / TEMPERATURE
        attn = jax.nn.softmax(scores, axis=-1)
        feats_att = jnp.matmul(attn, f)
        feats_fcm = f * W_BLEND + feats_att * (1.0 - W_BLEND)
        return _l2norm(feats_fcm.reshape(B, N, C))

    def _L0_ffn_ref(input_embeddings, router_w, w1, b1, w2, b2):
        import jax, jax.numpy as jnp
        import numpy as np
        NUM_EXPERTS = 8
        TOP_K = 2
        B, S, D = (8, 2048, 64)

        def _moe(tokens, router_w, w1, b1, w2, b2):
            N = tokens.shape[0]
            E = router_w.shape[0]
            logits = tokens.astype(jnp.float32) @ router_w.astype(jnp.float32).T
            probs = jax.nn.softmax(logits, axis=-1)
            rw, re = jax.lax.top_k(probs, TOP_K)
            if TOP_K > 1:
                rw = rw / jnp.maximum(rw.sum(-1, keepdims=True), 1e-12)
            rw = rw.astype(tokens.dtype)
            combine = jnp.zeros((N, E), tokens.dtype).at[jnp.arange(N)[:, None], re].set(rw)
            out = tokens
            for e in range(E):
                h = jax.nn.gelu(tokens @ w1[e] + b1[e], approximate=False)
                y = h @ w2[e] + b2[e]
                out = out + combine[:, e:e + 1] * y
            return out
        b, s, d = input_embeddings.shape
        tokens = input_embeddings.reshape(b * s, d)
        return _moe(tokens, router_w, w1, b1, w2, b2).reshape(b, s, d)
    h = _L0_tok_ref(x, L0_tok_W)
    h = _layernorm(h + _L0_attn_ref(h), axis=-1)
    h = _layernorm(h + _L0_ffn_ref(h, L0_ffn_router_w, L0_ffn_w1, L0_ffn_b1, L0_ffn_w2, L0_ffn_b2), axis=-1)
    return h

_drawn_inputs = setup_inputs


def setup_inputs(seed=0):
    import zlib

    import numpy as np

    out = dict(_drawn_inputs(seed))
    spreads = {'L0_ffn_b1': (0.0, 0.332), 'L0_ffn_b2': (0.0, 0.1)}
    factors = {}
    for name, (base, spread) in spreads.items():
        noise = np.random.default_rng([zlib.crc32(name.encode()), seed]).standard_normal(out[name].shape)
        drawn = base * np.exp(spread * noise) if base else spread * noise
        out[name] = jnp.asarray(drawn.astype(out[name].dtype))
    for name, factor in factors.items():
        out[name] = (out[name] * factor).astype(out[name].dtype)
    return out
```

```python
import math
from contextlib import ExitStack

import numpy as np

import concourse.bass as bass
from concourse import mybir

F32 = mybir.dt.float32
F16 = mybir.dt.float16
BF16 = mybir.dt.bfloat16
ALU = mybir.AluOpType
ACT = mybir.ActivationFunctionType
AX = mybir.AxisListType

B, C, T, V = 8, 64, 128, 64
PATCH, STRIDE = 16, 8
NP = (T + STRIDE - PATCH) // STRIDE + 1
NM = T // STRIDE
NF = 2 * (PATCH // 2 + 1)
D = 64
E = 8
HALF = STRIDE // 2
BP = B // 2
NT = BP * NP
NTOK = 128 * NT
QC = 1024
NQ = NTOK // QC
PAIRS = NT // 2
NPAIR = E // 2
G = 16
NG = NT // G
CH = 4
NCH = G // CH
WIDE = NPAIR * 128 + E + D
XR = 4
XLEN = NM * HALF * V


def constants():
    c = np.zeros((128, 128 + PATCH + NPAIR * 128 + E), np.float32)
    c[:, 0:128] = np.eye(128)
    for f in range(PATCH // 2 + 1):
        for p in range(PATCH):
            a = 2 * math.pi * f * p / PATCH
            c[f, 128 + p] = math.cos(a) / math.sqrt(PATCH)
            c[NF // 2 + f, 128 + p] = -math.sin(a) / math.sqrt(PATCH)
    at = 128 + PATCH
    for e in range(E):
        for part in range(2):
            c[part * E + e, at + 64 * e:at + 64 * e + 64] = 1.0
    c[:, at + NPAIR * 128:] = np.arange(E) - E
    return c


def tower(nc, x, W, router_w, w1, b1, w2, b2, consts, out):
    ctx = ExitStack()
    with ctx:
        def sb(name, shape, dt):
            return ctx.enter_context(nc.sbuf_tensor(name, shape, dt))

        def sem(name):
            return ctx.enter_context(nc.semaphore(name))

        cst = sb("cst", [128, 128 + PATCH + NPAIR * 128 + E], F32)
        ident = cst[:, 0:128]
        dft = cst[0:NF, 128:128 + PATCH]
        sel_f = cst[0:2 * E, 128 + PATCH:128 + PATCH + NPAIR * 128]
        enum = cst[:, 128 + PATCH + NPAIR * 128:]
        ident16 = sb("ident16", [128, 128], F16)
        sel = sb("sel", [2 * E, NPAIR * 128], F16)
        weff = sb("weff", [128, HALF, 128], F32)
        xedge = sb("xedge", [128, B, V], F32)

        ring = sb("ring", [128, XR * XLEN], F32)
        xring = ring[:, :].rearrange("p (r m s v) -> p r m s v", r=XR, m=NM, s=HALF)
        outT = ring[:, 0:NTOK]
        probs = ring[:, NTOK:NTOK + 4 * QC].rearrange("p (i q) -> p i q", i=4)
        probs_lo = ring[:, NTOK + 4 * QC:NTOK + 6 * QC].bitcast(F16).rearrange("p (i q) -> p i q", i=4)

        big = sb("big", [128, 3 * NTOK // 2], F32)
        prod = big[:, 0:B * (NM + 1) * V].rearrange("p (b m c v) -> p b m c v", b=BP, m=NM + 1, c=2)
        wg = ring[0:NF, 0:D * 128].rearrange("g (o k) -> g o k", o=D)
        fT = [big[:, i * NTOK // 2:(i + 1) * NTOK // 2].bitcast(F16) for i in range(3)]
        h = sb("h", [128, NT, D], F32)
        f = sb("f", [128, NT, D], F32)
        fs = sb("fs", [128, NT, 2 * D], F16)
        tmp = sb("tmp", [128, NT // 4, D], F32)
        stat = sb("stat", [128, 8, NT], F32)
        rowsum = sb("rowsum", [128, NQ * NT], F32)
        rtmp = sb("rtmp", [128, 10, G * E], F32)
        comb = sb("comb", [128, G, 2 * E], F16)
        wall = sb("wall", [128, WIDE], F32)
        wres = sb("wres", [128, 2, WIDE], F32)
        wp = sb("wp", [128, 3, WIDE], BF16)
        w2s = sb("w2s", [128, NPAIR, D], F32)
        b1s = sb("b1s", [128, NPAIR], F32)
        hT = fT[0]
        combT = sb("combT", [2 * E, 2, CH * 128], F16)
        hid = ring[:, 0:4 * 512].rearrange("p (i t) -> p i t", i=4)
        hidc = ring[:, 4 * 512:8 * 512].rearrange("p (i t) -> p i t", i=4)
        yT = ring[:, 8 * 512:10 * 512].rearrange("p (i t) -> p i t", i=2)

        ps = ctx.enter_context(nc.psum_tensor("ps", [128, 4096], F32))

        def bank(i, n=1):
            return ps[:, 512 * i:512 * (i + n)]

        s_cst, s_wg, s_x, s_xe, s_w, s_w1r = (sem(n) for n in ("s_cst", "s_wg", "s_x", "s_xe", "s_w", "s_w1r"))
        s_xb = [sem(f"s_x{i}") for i in range(XR)]
        s_id16, s_zero, s_split, s_wp = (sem(n) for n in ("s_id16", "s_zero", "s_split", "s_wp"))
        s_wfold, s_weff = sem("s_wfold"), sem("s_weff")
        s_prod, s_prodev, s_tr, s_h, s_pad, s_padev = (sem(n) for n in ("s_prod", "s_prodev", "s_tr", "s_h", "s_pad", "s_padev"))
        s_ss, s_rt, s_fs, s_ftr, s_ftev, s_ftev2 = (sem(n) for n in ("s_ss", "s_rt", "s_fs", "s_ftr", "s_ftev", "s_ftev2"))
        s_sc, s_pr, s_lo, s_pv, s_oev = (sem(n) for n in ("s_sc", "s_pr", "s_lo", "s_pv", "s_oev"))
        s_at, s_atr, s_sq1, s_rt1, s_sq2, s_rt2, s_hs = (sem(n) for n in ("s_at", "s_atr", "s_sq1", "s_rt1", "s_sq2", "s_rt2", "s_hs"))
        s_sqd1, s_sqd2 = sem("s_sqd1"), sem("s_sqd2")
        s_htr, s_htev, s_lg, s_ctr, s_cev, s_comb = (sem(n) for n in ("s_htr", "s_htev", "s_lg", "s_ctr", "s_cev", "s_comb"))
        s_lgr, s_exp = sem("s_lgr"), sem("s_exp")
        s_up, s_gelu, s_ex, s_hc, s_dn, s_yev, s_ytr, s_y = (sem(n) for n in ("s_up", "s_gelu", "s_ex", "s_hc", "s_dn", "s_yev", "s_ytr", "s_y"))
        s_sq3, s_sqd3, s_rt3, s_fin, s_out = (sem(n) for n in ("s_sq3", "s_sqd3", "s_rt3", "s_fin", "s_out"))
        s_ch = [sem(f"s_ch{i}") for i in range(6)]

        block = ctx.enter_context(nc.Block())

        def chained(eng, s, base=0):
            n = [0]

            def then(ins):
                n[0] += 1
                ins.then_inc(s, 1)
                eng.wait_ge(s, base + n[0])
            return then

        x_h = x.rearrange("b c (m h s) v -> b h c m (s v)", m=NM, h=2)
        out_t = out.rearrange("(bp b2) (v n) o -> bp b2 v n o", b2=2, n=NP)

        @block.sync
        def _(sp):
            sp.dma_start(cst[:, :], consts).then_inc(s_cst, 16)
            for half in range(2):
                sp.dma_start(wg[:, :, 64 * half:64 * half + 64],
                             W.rearrange("o (g c) -> g o c", c=C)).then_inc(s_wg, 16)
            for b in range(B):
                for half in range(2):
                    if b >= XR:
                        sp.wait_ge(s_prod, b - XR + 1)
                    if b == 0 and half == 0:
                        sp.wait_ge(s_wfold, 1)
                    sp.dma_start(xring[64 * half:64 * half + 64, b % XR, :, :, :].rearrange("p m s v -> p m (s v)"),
                                 x_h[b, half]).then_inc(s_xb[b % XR], 16)
            for g in range(NG):
                sp.wait_ge(s_fin, g + 1)
                for b2 in range(2):
                    sp.dma_start(out_t[g, b2], h[64 * b2:64 * b2 + 64, g * G:(g + 1) * G, :]).then_inc(s_out, 16)
            sp.wait_ge(s_out, 16 * 2 * NG)

        @block.gpsimd
        def _(pool):
            pool.memset(wall[:, :], 0.0).then_inc(s_zero, 1)
            pool.wait_ge(s_zero, 1)
            for half in range(2):
                rows = slice(64 * half, 64 * half + 64)
                pool.dma_start(xedge[rows], x[:, :, T - 1, :].rearrange("b c v -> c b v")).then_inc(s_xe, 16)
                pool.dma_start(wall[rows, 0:512].rearrange("p (e k) -> p e k", e=E),
                               w1.rearrange("e d k -> d e k")).then_inc(s_w, 16)
                with nc.allow_non_contiguous_dma(reason="512 floats"):
                    pool.dma_start(wall[rows, 512:512 + E], router_w.rearrange("e d -> d e")).then_inc(s_w, 16)
                pool.dma_start(wall[half * E:half * E + E, 512 + E:], b2).then_inc(s_w, 16)
                pool.dma_start(w2s[rows], w2[half:E:2].rearrange("i k o -> k i o")).then_inc(s_w1r, 16)
                with nc.allow_non_contiguous_dma(reason="512 floats"):
                    pool.dma_start(b1s[rows], b1[half:E:2].rearrange("i k -> k i")).then_inc(s_w1r, 16)
            pool.wait_ge(s_cst, 16)
            nc.gpsimd.tensor_copy(ident16[:, :], ident).then_inc(s_id16, 1)
            nc.gpsimd.tensor_copy(sel[:, :], sel_f).then_inc(s_id16, 1)
            pool.wait_ge(s_w, 96)
            then = chained(pool, s_split)
            then(nc.gpsimd.tensor_copy(wp[:, 0, :], wall[:, :]))
            then(nc.gpsimd.tensor_tensor(wres[:, 0, :], wall[:, :], wp[:, 0, :], ALU.subtract))
            then(nc.gpsimd.tensor_copy(wp[:, 1, :], wres[:, 0, :]))
            then(nc.gpsimd.tensor_tensor(wres[:, 1, :], wres[:, 0, :], wp[:, 1, :], ALU.subtract))
            nc.gpsimd.tensor_copy(wp[:, 2, :], wres[:, 1, :]).then_inc(s_wp, 1)

        @block.tensor
        def _(pe):
            mm = nc.tensor.matmul
            pe.wait_ge(s_cst, 16)
            pe.wait_ge(s_wg, 32)
            for o in range(D):
                last = mm(bank(o * PATCH // 512)[:, o * PATCH % 512:o * PATCH % 512 + PATCH],
                          wg[:, o, :], dft, start=True, stop=True)
            last.then_inc(s_wfold, 1)
            pe.wait_ge(s_weff, 2)

            def products(b):
                pe.wait_ge(s_xb[b % XR], 32 * (b // XR + 1))
                if b >= 2:
                    pe.wait_ge(s_prodev, b - 1)
                for q in range(2):
                    for s in range(HALF):
                        last = mm(bank(2 * (b % 2) + q).rearrange("p (m v) -> p m v", v=V), weff[:, s, :],
                                  xring[:, b % XR, 8 * q:8 * q + 8, s, :], start=(s == 0), stop=(s == HALF - 1))
                last.then_inc(s_prod, 1)

            def tokens(i):
                bp, n0 = i // 2, 8 * (i % 2)
                pe.wait_ge(s_prodev, 2 * bp + 2)
                if i == 0:
                    pe.wait_ge(s_padev, 1)
                if i >= 2:
                    pe.wait_ge(s_h, i - 1)
                for k in range(8):
                    for s in range(2):
                        last = mm(bank(4 + 2 * (i % 2) + s)[:, 64 * k:64 * k + 64],
                                  prod[64 * s:64 * s + 64, bp, n0 + k + s, :, :].rearrange("p c v -> p (c v)"),
                                  ident[64 * s:64 * s + 64, 64 * s:64 * s + 64], is_transpose=True, start=True, stop=True)
                last.then_inc(s_tr, 1)

            pe.wait_ge(s_xe, 32)
            for s in range(HALF):
                last = mm(bank(7).rearrange("p (b v) -> p b v", v=V), weff[:, s, :], xedge[:, :, :],
                          start=(s == 0), stop=(s == HALF - 1))
            last.then_inc(s_pad, 1)
            for b in range(B):
                products(b)
                if b >= 2 and b % 2 == 0:
                    tokens(b - 2)
                    tokens(b - 1)
            for i in (B - 2, B - 1):
                tokens(i)
            pe.wait_ge(s_id16, 2)
            pe.wait_ge(s_prodev, B)
            for i in range(NT // 8):
                pe.wait_ge(s_fs, i // 2 + 1)
                if i == 1:
                    pe.wait_ge(s_h, 2 * BP)
                if i >= 2:
                    pe.wait_ge(s_ftev, i - 1)
                    pe.wait_ge(s_ftev2, 2 * (i - 1))
                for kind in range(3):
                    dst = bank(3 * (i % 2) + kind).bitcast(F16)
                    for k in range(8):
                        j = 8 * i + k
                        if kind == 0:
                            last = mm(dst[:, 128 * k:128 * k + 128], fs[:, j, :], ident16[:, :], is_transpose=True,
                                      start=True, stop=True)
                        else:
                            for rows in (0, 64):
                                last = mm(dst[rows:rows + 64, 128 * k:128 * k + 128],
                                          fs[:, j, 64 * (kind - 1):64 * kind], ident16[:, :], is_transpose=True,
                                          start=True, stop=True)
                last.then_inc(s_ftr, 1)

            def scores(k, q0):
                for half in range(2):
                    for i in (1, 2):
                        last = mm(bank(2 * (k % 2) + half), fT[0][:, 128 * k:128 * k + 128],
                                  fT[i][:, bass.ds(q0 + 512 * half, 512)], start=(i == 1), stop=(i == 2))
                last.then_inc(s_sc, 1)

            def weighted(t, first_probs):
                pe.wait_ge(s_pr, first_probs + 2 * t + 2)
                for e in range(2):
                    k = 2 * t + e
                    for half in range(2):
                        mm(bank(4 + half), fs[:, k, :],
                           probs[:, 2 * (t % 2) + e, :].bitcast(BF16)[:, 1024 * half + 1:1024 * half + 1024:2],
                           start=(k == 0), stop=False, skip_group_check=True)
                pe.wait_ge(s_lo, first_probs + 2 * t + 2)
                for half in range(2):
                    for e in range(2):
                        k = 2 * t + e
                        last = mm(bank(4 + half)[64 * e:64 * e + 64, :], fs[:, k, 0:64],
                                  probs_lo[:, 2 * (t % 2) + e, 512 * half:512 * half + 512],
                                  start=False, stop=(k >= NT - 2), skip_group_check=True)
                last.then_inc(s_pv, 1)
                return last

            pe.wait_ge(s_ftev, NT // 8)
            pe.wait_ge(s_ftev2, 2 * (NT // 8))
            scores(0, 0)
            scores(1, 0)

            def chunk(q, last_chunk):
                for t in range(PAIRS):
                    if t < PAIRS - 1 or not last_chunk:
                        nk, nq = (2 * t + 2, q * QC) if t < PAIRS - 1 else (0, (q + 1) * QC)
                        for e in range(2):
                            pe.wait_ge(s_pr, q * NT + 2 * t + 1 + e)
                            scores(nk + e, nq)
                    if t == 0 and not (isinstance(q, int) and q == 0):
                        pe.wait_ge(s_oev, q)
                    weighted(t, q * NT)

            chunk(0, False)
            with pe.Fori(1, NQ - 1) as q:
                chunk(q, False)
            chunk(NQ - 1, True)

            pe.wait_ge(s_oev, NQ)
            for i in range(NT // 8):
                if i >= 2:
                    pe.wait_ge(s_atr, i - 1)
                for k in range(8):
                    j = 8 * i + k
                    last = mm(ps[:, 1024 * (i % 2) + 128 * k:1024 * (i % 2) + 128 * k + 128],
                              outT[:, 128 * j:128 * j + 128], ident, is_transpose=True, start=True, stop=True)
                last.then_inc(s_at, 1)

            pe.wait_ge(s_wp, 1)
            pe.wait_ge(s_w1r, 64)
            for g in range(NG):
                pe.wait_ge(s_hs, g + 1)
                if g == 0:
                    pe.wait_ge(s_atr, NT // 8)
                else:
                    pe.wait_ge(s_lgr, g)
                for i in range(G // 8):
                    n = g * (G // 8) + i
                    if n >= 1:
                        pe.wait_ge(s_htev, n)
                    for k in range(8):
                        j = g * G + 8 * i + k
                        last = mm(bank(0).bitcast(F16)[:, 128 * k:128 * k + 128], fs[:, j, :], ident16[:, :],
                                  is_transpose=True, start=True, stop=True)
                    last.then_inc(s_htr, 1)
                pe.wait_ge(s_htev, (g + 1) * (G // 8))
                for k in range(G):
                    j = g * G + k
                    for part in range(3):
                        last = mm(bank(1)[:, 256 + E * k:256 + E * k + E], hT[:, 128 * j:128 * j + 128],
                                  wp[:, part, 512:512 + E], start=(part == 0), stop=(part == 2))
                last.then_inc(s_lg, 1)
                pe.wait_ge(s_comb, g + 1)
                for c in range(NCH):
                    n = g * NCH + c
                    if n >= 1:
                        pe.wait_ge(s_cev, n)
                    for k in range(CH):
                        last = mm(bank(1).bitcast(F16)[0:2 * E, 128 * k:128 * k + 128], comb[:, CH * c + k, :],
                                  ident16[:, :], is_transpose=True, start=True, stop=True)
                    last.then_inc(s_ctr, 1)
                    pe.wait_ge(s_cev, n + 1)
                    t0 = 512 * n
                    for i in range(NPAIR):
                        u = n * NPAIR + i
                        if u >= 2:
                            pe.wait_ge(s_gelu, u - 1)
                        for part in range(3):
                            last = mm(bank(2 + u % 2), wp[:, part, 128 * i:128 * i + 128], hT[:, t0:t0 + 512],
                                      start=(part == 0), stop=(part == 2))
                        last.then_inc(s_up, 1)
                        if u >= 2:
                            pe.wait_ge(s_hc, u - 1)
                        mm(bank(4 + u % 2), sel[:, 128 * i:128 * i + 128], combT[:, n % 2, :],
                           start=True, stop=True).then_inc(s_ex, 1)
                    if n >= 1:
                        pe.wait_ge(s_yev, n)
                    for part in range(3):
                        mm(bank(6)[0:64, :], wp[0:2 * E, part, 512 + E:], combT[:, n % 2, :],
                           start=(part == 0), stop=False, skip_group_check=True)
                    for i in range(NPAIR):
                        pe.wait_ge(s_hc, n * NPAIR + i + 1)
                        e = i % 2
                        last = mm(bank(6)[64 * e:64 * e + 64, :], w2s[:, i, :], hidc[:, i, :],
                                  start=(i == 1), stop=(i >= 2), skip_group_check=True)
                    last.then_inc(s_dn, 1)
                    pe.wait_ge(s_yev, n + 1)
                    if n >= 1:
                        pe.wait_ge(s_y, n)
                    for k in range(CH):
                        last = mm(bank(7)[:, 128 * k:128 * k + 128], yT[:, n % 2, 128 * k:128 * k + 128], ident,
                                  is_transpose=True, start=True, stop=True)
                    last.then_inc(s_ytr, 1)

        @block.scalar
        def _(act):
            a = nc.scalar.activation
            act.wait_ge(s_wfold, 1)
            fold = ps[:, 0:1024].rearrange("p (o s h t) -> p h t s o", o=D, s=2, h=2)
            for s in range(2):
                last = a(weff[64:128, :, 64 * s:64 * s + 64], fold[64:128, 1, :, s, :], ACT.Copy)
            last.then_inc(s_weff, 1)
            act.wait_ge(s_pad, 1)
            a(prod[:, :, NM, :, :], bank(7).rearrange("p (b c v) -> p b c v", c=2, v=V), ACT.Copy).then_inc(s_padev, 1)
            def root(g):
                act.wait_ge(s_ss, g + 1)
                a(stat[:, 1, G * g:G * g + G], stat[:, 0, G * g:G * g + G], ACT.Sqrt).then_inc(s_rt, 1)

            for b in range(B):
                act.wait_ge(s_prod, b + 1)
                a(prod[:, b // 2, 0:NM, b % 2, :], bank(2 * (b % 2), 2).rearrange("p (m v) -> p m v", v=V),
                  ACT.Copy).then_inc(s_prodev, 1)
                if b >= 3 and b % 2:
                    root((b - 3) // 2)
            root(BP - 1)
            for i in range(NT // 8):
                act.wait_ge(s_ftr, i + 1)
                a(fT[2][:, 1024 * i:1024 * i + 1024], bank(3 * (i % 2) + 2).bitcast(F16)[:, 0:1024],
                  ACT.Copy).then_inc(s_ftev, 1)

            def exps(q, first):
                for k in range(NT):
                    act.wait_ge(s_sc, q * NT + k + 1)
                    if not (first and k < 4):
                        act.wait_ge(s_pv, q * PAIRS + k // 2 - 1)
                    a(probs[:, k % 4, :], bank(2 * (k % 2), 2), ACT.Exp,
                      accum_out=rowsum[:, bass.ds(q * NT + k, 1)]).then_inc(s_pr, 1)
            exps(0, True)
            with act.Fori(1, NQ) as q:
                exps(q, False)

            for g in range(NG):
                sl = slice(g * G, g * G + G)
                act.wait_ge(s_sq1, g + 1)
                a(tmp[:, :, :], f[:, sl, :], ACT.Square).then_inc(s_sqd1, 1)
                act.wait_ge(s_rt1, 2 * g + 1)
                a(stat[:, 1, sl], stat[:, 0, sl], ACT.Sqrt).then_inc(s_rt2, 1)
                act.wait_ge(s_sq2, g + 1)
                a(tmp[:, :, :], h[:, sl, :], ACT.Square).then_inc(s_sqd2, 1)
                act.wait_ge(s_rt1, 2 * g + 2)
                a(stat[:, 3, sl], stat[:, 2, sl], ACT.Sqrt).then_inc(s_rt2, 1)
            for g in range(NG):
                sl = slice(g * G, g * G + G)
                act.wait_ge(s_lgr, g + 1)
                a(rtmp[:, 1, :], rtmp[:, 0, :], ACT.Exp).then_inc(s_exp, 1)
                for c in range(NCH):
                    n = g * NCH + c
                    act.wait_ge(s_ctr, n + 1)
                    if n >= 2:
                        act.wait_ge(s_dn, n - 1)
                    a(combT[:, n % 2, :], bank(1).bitcast(F16)[0:2 * E, 0:512], ACT.Copy).then_inc(s_cev, 1)
                    for i in range(NPAIR):
                        u = n * NPAIR + i
                        act.wait_ge(s_up, u + 1)
                        if u >= 4:
                            act.wait_ge(s_hc, u - 3)
                        a(hid[:, i, :], bank(2 + u % 2), ACT.Gelu, bias=b1s[:, i:i + 1]).then_inc(s_gelu, 1)
                    act.wait_ge(s_dn, n + 1)
                    if n >= 2:
                        act.wait_ge(s_ytr, n - 1)
                    a(yT[:, n % 2, :], bank(6), ACT.Copy).then_inc(s_yev, 1)
                act.wait_ge(s_sq3, 2 * g + 1)
                a(tmp[:, :, :], h[:, sl, :], ACT.Square).then_inc(s_sqd3, 1)
                act.wait_ge(s_sq3, 2 * g + 2)
                a(stat[:, 3, sl], stat[:, 2, sl], ACT.Sqrt).then_inc(s_rt3, 1)

        @block.vector
        def _(dve):
            tt, ts, cp, red = nc.vector.tensor_tensor, nc.vector.tensor_scalar, nc.vector.tensor_copy, nc.vector.tensor_reduce
            stt = nc.vector.scalar_tensor_tensor

            def wide(v, n, d=D):
                return v.unsqueeze(2).to_broadcast([128, n, d])

            dve.wait_ge(s_wfold, 1)
            fold = ps[:, 0:1024].rearrange("p (o s h t) -> p h t s o", o=D, s=2, h=2)
            for s in range(2):
                last = cp(weff[0:64, :, 64 * s:64 * s + 64], fold[0:64, 0, :, s, :])
            last.then_inc(s_weff, 1)
            then = chained(dve, s_ch[0])
            for g in range(BP):
                sl = slice(g * G, g * G + G)
                for i in (2 * g, 2 * g + 1):
                    dve.wait_ge(s_tr, i + 1)
                    red(h[:, 8 * i:8 * i + 8, :],
                        bank(4 + 2 * (i % 2), 2).rearrange("p (s n o) -> p n o s", s=2, o=D),
                        AX.X, ALU.add).then_inc(s_h, 1)
                dve.wait_ge(s_h, 2 * g + 2)
                then(tt(tmp[:, :, :], h[:, sl, :], h[:, sl, :], ALU.mult))
                red(stat[:, 0, sl], tmp[:, :, :], AX.X, ALU.add).then_inc(s_ss, 1)
                dve.wait_ge(s_rt, g + 1)
                then(ts(stat[:, 2, sl], stat[:, 1, sl], 1e-12, None, ALU.max))
                then(nc.vector.reciprocal(stat[:, 3, sl], stat[:, 2, sl]))
                then(tt(f[:, sl, :], h[:, sl, :], wide(stat[:, 3, sl], G), ALU.mult))
                then(cp(fs[:, sl, 0:D], f[:, sl, :]))
                tt(fs[:, sl, D:2 * D], f[:, sl, :], fs[:, sl, 0:D], ALU.subtract).then_inc(s_fs, 1)
            dve.wait_ge(s_prodev, B)
            for i in range(NT // 8):
                dve.wait_ge(s_ftr, i + 1)
                for kind in range(2):
                    cp(fT[kind][:, 1024 * i:1024 * i + 1024],
                       bank(3 * (i % 2) + kind).bitcast(F16)[:, 0:1024]).then_inc(s_ftev2, 1)

            def low_parts(q, first):
                for k in range(NT):
                    dve.wait_ge(s_pr, q * NT + k + 1)
                    if not (first and k < 4):
                        dve.wait_ge(s_pv, q * PAIRS + k // 2 - 1)
                    tt(probs_lo[:, k % 4, :], probs[:, k % 4, :], probs[:, k % 4, :].bitcast(BF16)[:, 1:2 * QC:2],
                       ALU.subtract).then_inc(s_lo, 1)
                    if k == 0 and not first:
                        sums_out(q - 1)

            def sums_out(q):
                dve.wait_ge(s_pv, (q + 1) * PAIRS)
                cp(outT[:, bass.ds(q * QC, QC)], bank(4, 2)).then_inc(s_oev, 1)

            low_parts(0, True)
            with dve.Fori(1, NQ) as q:
                low_parts(q, False)
            sums_out(NQ - 1)

            then = chained(dve, s_ch[1])
            dve.wait_ge(s_pr, NQ * NT)
            then(red(stat[:, 4, :], rowsum[:, :].rearrange("p (q k) -> p k q", q=NQ), AX.X, ALU.add))
            then(nc.vector.reciprocal(stat[:, 5, :], stat[:, 4, :]))
            then(ts(stat[:, 6, :], stat[:, 5, :], 1.0 - 0.8, None, ALU.mult))
            att = tmp
            for g in range(NG):
                sl = slice(g * G, g * G + G)
                for i in range(2):
                    n = 2 * g + i
                    dve.wait_ge(s_at, n + 1)
                    if n == 0:
                        dve.wait_ge(s_lo, 1)
                    r = red(att[:, 8 * i:8 * i + 8, :],
                            ps[:, 1024 * (n % 2):1024 * (n % 2) + 1024].rearrange("p (j s o) -> p j o s", s=2, o=D),
                            AX.X, ALU.add)
                    r.then_inc(s_atr, 1)
                dve.wait_ge(s_atr, 2 * g + 2)
                then(tt(att[:, :, :], att[:, :, :], wide(stat[:, 6, sl], G), ALU.mult))
                stt(f[:, sl, :], f[:, sl, :], 0.8, att[:, :, :], ALU.mult, ALU.add).then_inc(s_sq1, 1)
                dve.wait_ge(s_sqd1, g + 1)
                red(stat[:, 0, sl], tmp[:, :, :], AX.X, ALU.add).then_inc(s_rt1, 1)
                dve.wait_ge(s_rt2, 2 * g + 1)
                then(ts(stat[:, 2, sl], stat[:, 1, sl], 1e-12, None, ALU.max))
                then(nc.vector.reciprocal(stat[:, 3, sl], stat[:, 2, sl]))
                then(tt(f[:, sl, :], f[:, sl, :], wide(stat[:, 3, sl], G), ALU.mult))
                then(tt(h[:, sl, :], h[:, sl, :], f[:, sl, :], ALU.add))
                then(red(stat[:, 0, sl], h[:, sl, :], AX.X, ALU.add))
                then(ts(stat[:, 1, sl], stat[:, 0, sl], 1.0 / D, None, ALU.mult))
                tt(h[:, sl, :], h[:, sl, :], wide(stat[:, 1, sl], G), ALU.subtract).then_inc(s_sq2, 1)
                dve.wait_ge(s_sqd2, g + 1)
                then(red(stat[:, 0, sl], tmp[:, :, :], AX.X, ALU.add))
                ts(stat[:, 2, sl], stat[:, 0, sl], 1.0 / D, 1e-5, ALU.mult, ALU.add).then_inc(s_rt1, 1)
                dve.wait_ge(s_rt2, 2 * g + 2)
                then(nc.vector.reciprocal(stat[:, 1, sl], stat[:, 3, sl]))
                then(tt(h[:, sl, :], h[:, sl, :], wide(stat[:, 1, sl], G), ALU.mult))
                then(cp(fs[:, sl, 0:D], h[:, sl, :]))
                tt(fs[:, sl, D:2 * D], h[:, sl, :], fs[:, sl, 0:D], ALU.subtract).then_inc(s_hs, 1)

            then = chained(dve, s_ch[2])
            for g in range(NG):
                sl = slice(g * G, g * G + G)
                for i in range(G // 8):
                    n = g * (G // 8) + i
                    dve.wait_ge(s_htr, n + 1)
                    cp(hT[:, 1024 * n:1024 * n + 1024], bank(0).bitcast(F16)[:, 0:1024]).then_inc(s_htev, 1)
                R = [rtmp[:, i, :] for i in range(10)]

                def by_tile(v):
                    return v.rearrange("p (t e) -> p t e", e=E)

                def per_tile(i):
                    return stat[:, i, 0:G]

                numbers = enum.unsqueeze(1).to_broadcast([128, G, E])
                dve.wait_ge(s_lg, g + 1)
                logits = bank(1)[:, 256:256 + G * E]
                then(red(per_tile(5), by_tile(logits), AX.X, ALU.max))
                tt(by_tile(R[0]), by_tile(logits), wide(per_tile(5), G, E), ALU.subtract).then_inc(s_lgr, 1)
                dve.wait_ge(s_exp, g + 1)
                then(red(per_tile(6), by_tile(R[1]), AX.X, ALU.add))
                then(nc.vector.reciprocal(per_tile(7), per_tile(6)))
                then(tt(by_tile(R[2]), by_tile(R[1]), wide(per_tile(7), G, E), ALU.mult))
                p, left = R[2], R[2]
                for rank in range(2):
                    eq, cand, one, pick = R[3], R[4], R[5 + rank], R[7 + rank]
                    then(red(per_tile(5), by_tile(left), AX.X, ALU.max))
                    then(tt(by_tile(eq), by_tile(left), wide(per_tile(5), G, E), ALU.is_equal))
                    then(tt(by_tile(cand), by_tile(eq), numbers, ALU.mult))
                    then(red(per_tile(6), by_tile(cand), AX.X, ALU.min))
                    then(tt(by_tile(one), numbers, wide(per_tile(6), G, E), ALU.is_equal))
                    then(tt(by_tile(pick), by_tile(p), by_tile(one), ALU.mult))
                    if rank == 0:
                        then(stt(R[9], one, -2.0, p, ALU.mult, ALU.add))
                        left = R[9]
                then(tt(R[3], R[7], R[8], ALU.add))
                then(red(per_tile(5), by_tile(R[3]), AX.X, ALU.add))
                then(ts(per_tile(6), per_tile(5), 1e-12, None, ALU.max))
                then(nc.vector.reciprocal(per_tile(7), per_tile(6)))
                if g >= 1:
                    dve.wait_ge(s_ctr, g * NCH)
                then(tt(by_tile(R[4]), by_tile(R[3]), wide(per_tile(7), G, E), ALU.mult))
                then(cp(comb[:, :, 0:E], by_tile(R[4])))
                tt(comb[:, :, E:2 * E], by_tile(R[4]), comb[:, :, 0:E], ALU.subtract).then_inc(s_comb, 1)
                for c in range(NCH):
                    n = g * NCH + c
                    for i in range(NPAIR):
                        u = n * NPAIR + i
                        dve.wait_ge(s_gelu, u + 1)
                        dve.wait_ge(s_ex, u + 1)
                        if n >= 1:
                            dve.wait_ge(s_dn, n)
                        tt(hidc[:, i, :], hid[:, i, :], bank(4 + u % 2), ALU.mult).then_inc(s_hc, 1)
                    dve.wait_ge(s_ytr, n + 1)
                    t4 = slice(CH * c, CH * c + CH)
                    if c == 0 and g > 0:
                        dve.wait_ge(s_sqd3, g)
                    red(f[:, n * CH:n * CH + CH, :], bank(7).rearrange("p (j s o) -> p j o s", s=2, o=D),
                        AX.X, ALU.add).then_inc(s_y, 1)
                dve.wait_ge(s_y, (g + 1) * NCH)
                then(stt(h[:, sl, :], h[:, sl, :], 2.0, f[:, sl, :], ALU.mult, ALU.add))
                then(red(stat[:, 0, sl], h[:, sl, :], AX.X, ALU.add))
                then(ts(stat[:, 1, sl], stat[:, 0, sl], 1.0 / D, None, ALU.mult))
                tt(h[:, sl, :], h[:, sl, :], wide(stat[:, 1, sl], G), ALU.subtract).then_inc(s_sq3, 1)
                dve.wait_ge(s_sqd3, g + 1)
                then(red(stat[:, 0, sl], tmp[:, :, :], AX.X, ALU.add))
                ts(stat[:, 2, sl], stat[:, 0, sl], 1.0 / D, 1e-5, ALU.mult, ALU.add).then_inc(s_sq3, 1)
                dve.wait_ge(s_rt3, g + 1)
                then(nc.vector.reciprocal(stat[:, 1, sl], stat[:, 3, sl]))
                tt(h[:, sl, :], h[:, sl, :], wide(stat[:, 1, sl], G), ALU.mult).then_inc(s_fin, 1)


_INS = ["x", "L0_tok_W", "L0_ffn_router_w", "L0_ffn_w1", "L0_ffn_b1", "L0_ffn_w2", "L0_ffn_b2"]


def kernel(**inputs):
    import numpy as _np
    import concourse.bacc as _bacc
    from concourse import mybir as _mybir
    from concourse.bass_utils import run_bass_kernel_spmd as _run

    nc = _bacc.Bacc("TRN2", target_bir_lowering=False, num_devices=1)
    arrays, args = {}, []
    for name in _INS:
        a = _np.ascontiguousarray(inputs[name])
        arrays[f"in_{name}_dram"] = a
        args.append(nc.dram_tensor(f"in_{name}_dram", a.shape, _mybir.dt.from_np(a.dtype), kind="ExternalInput").ap())
    c = constants()
    arrays["consts_dram"] = c
    args.append(nc.dram_tensor("consts_dram", c.shape, _mybir.dt.from_np(c.dtype), kind="ExternalInput").ap())
    args.append(nc.dram_tensor("out_dram", (B, V * NP, D), _mybir.dt.float32, kind="ExternalOutput").ap())
    tower(nc, *args)
    r = _run(nc, [arrays], core_ids=[0])
    return r.results[0]["out_dram"]
```

```python
import math
from contextlib import ExitStack

import numpy as np

import concourse.bass as bass
from concourse import mybir

F32 = mybir.dt.float32
F16 = mybir.dt.float16
BF16 = mybir.dt.bfloat16
ALU = mybir.AluOpType
ACT = mybir.ActivationFunctionType
AX = mybir.AxisListType

B, C, T, V = 8, 64, 128, 64
PATCH, STRIDE = 16, 8
NP = (T + STRIDE - PATCH) // STRIDE + 1
NM = T // STRIDE
NF = 2 * (PATCH // 2 + 1)
D = 64
E = 8
HALF = STRIDE // 2
BP = B // 2
NT = BP * NP
NTOK = 128 * NT
QC = 1024
NQ = NTOK // QC
PAIRS = NT // 2
NPAIR = E // 2
HG = NT // BP
G = 8
NG = NT // G
CH = 4
NCH = G // CH
WIDE = NPAIR * 128 + E + D
XR = 4
XLEN = NM * HALF * V
CONSTS = 128 + HALF * NF + NPAIR * 128 + E + D + G


def constants():
    c = np.zeros((128, CONSTS), np.float32)
    c[:, 0:128] = np.eye(128)
    for half in range(2):
        for s in range(HALF):
            for f in range(PATCH // 2 + 1):
                a = 2 * math.pi * f * (HALF * half + s) / PATCH
                c[64 * half:64 * half + 64, 128 + NF * s + f] = math.cos(a) / math.sqrt(PATCH)
                c[64 * half:64 * half + 64, 128 + NF * s + NF // 2 + f] = -math.sin(a) / math.sqrt(PATCH)
    at = 128 + HALF * NF
    for e in range(E):
        for part in range(2):
            c[part * E + e, at + 64 * e:at + 64 * e + 64] = 1.0
    at += NPAIR * 128
    c[:, at:at + E] = np.arange(E) - E
    at += E
    for row in range(128):
        c[row, at + row % 64] = 1.0
    c[:, at + D:at + D + G] = -0.5
    return c


def tower(nc, x, W, router_w, w1, b1, w2, b2, consts, out):
    ctx = ExitStack()
    with ctx:
        def sb(name, shape, dt):
            return ctx.enter_context(nc.sbuf_tensor(name, shape, dt))

        def sem(name):
            return ctx.enter_context(nc.semaphore(name))

        cst = sb("cst", [128, CONSTS], F32)
        ident = cst[:, 0:128]
        dft = cst[:, 128:128 + HALF * NF].rearrange("p (s g) -> p s g", s=HALF)
        at = 128 + HALF * NF
        sel_f = cst[0:2 * E, at:at + NPAIR * 128]
        enum = cst[:, at + NPAIR * 128:at + NPAIR * 128 + E]
        at += NPAIR * 128 + E
        both = cst[:, at:at + D]
        minus_half = cst[:, at + D:at + D + G]
        ident16 = sb("ident16", [128, 128], F16)
        sel = sb("sel", [2 * E, NPAIR * 128], F16)
        weff = sb("weff", [128, HALF, 128], F32)
        xedge = sb("xedge", [128, B, V], F32)

        ring = sb("ring", [128, XR * XLEN], F32)
        xring = ring[:, :].rearrange("p (r m s v) -> p r m s v", r=XR, m=NM, s=HALF)
        outT = ring[:, 0:NTOK]
        probs = ring[:, NTOK:NTOK + 4 * QC].rearrange("p (i q) -> p i q", i=4)
        probs_lo = ring[:, NTOK + 4 * QC:NTOK + 6 * QC].bitcast(F16).rearrange("p (i q) -> p i q", i=4)

        big = sb("big", [128, 3 * NTOK // 2], F32)
        prod = big[:, 0:B * (NM + 1) * V].rearrange("p (b m c v) -> p b m c v", b=BP, m=NM + 1, c=2)
        fT = [big[:, i * NTOK // 2:(i + 1) * NTOK // 2].bitcast(F16) for i in range(3)]
        h = sb("h", [128, NT, D], F32)
        f = sb("f", [128, NT, D], F32)
        wraw = f[0:D, 0:2 * NF, :].rearrange("o (g h) c -> o g h c", h=2)
        wdft = [h[:, NF * s:NF * s + NF, :] for s in range(3)] + \
               [big[:, B * (NM + 1) * V:B * (NM + 1) * V + NF * D].rearrange("p (g o) -> p g o", o=D)]
        fs = sb("fs", [128, NT, 2 * D], F16)
        wpar = sb("wpar", [128, 2, HALF, D], F32)
        tmp = sb("tmp", [128, HG, D], F32)
        stat = sb("stat", [128, 8, NT], F32)
        rowsum = sb("rowsum", [128, NQ * NT], F32)
        rtmp = sb("rtmp", [128, 12, G * E], F32)
        wall = sb("wall", [128, WIDE], F32)
        wres = sb("wres", [128, 2, WIDE], F32)
        wp = sb("wp", [128, 3, WIDE], BF16)
        w2s = sb("w2s", [128, NPAIR, D], F32)
        b1s = sb("b1s", [128, NPAIR], F32)
        hT = fT[0]
        combT = sb("combT", [2 * E, 2, G * 128], F16)
        late = ring[:, NTOK:NTOK + 15 * 512].rearrange("p (i t) -> p i t", t=512)
        hid, hidc, yT, att = late[:, 0:4], late[:, 4:8], late[:, 8:10], late[:, 10]
        sq_g, sq_h, sq_o = (late[:, 11 + i, :].rearrange("p (j o) -> p j o", o=D) for i in range(3))
        combine = late[:, 14, :].bitcast(F16)[:, 0:2 * G * 2 * E].rearrange("p (i j e) -> p i j e", i=2, e=2 * E)

        ps = ctx.enter_context(nc.psum_tensor("ps", [128, 4096], F32))

        def bank(i, n=1):
            return ps[:, 512 * i:512 * (i + n)]

        s_cst, s_wg, s_x, s_xe, s_w, s_w1r = (sem(n) for n in ("s_cst", "s_wg", "s_x", "s_xe", "s_w", "s_w1r"))
        s_xb = [sem(f"s_x{i}") for i in range(XR)]
        s_id16, s_zero, s_split, s_wp = (sem(n) for n in ("s_id16", "s_zero", "s_split", "s_wp"))
        s_wfold, s_weff, s_fold, s_sqf, s_sqfd, s_hi = (sem(n) for n in ("s_wfold", "s_weff", "s_fold", "s_sqf", "s_sqfd", "s_hi"))
        s_prod, s_prodev, s_tr, s_h, s_pad, s_padev = (sem(n) for n in ("s_prod", "s_prodev", "s_tr", "s_h", "s_pad", "s_padev"))
        s_ss, s_rt, s_fs, s_ftr, s_ftev, s_ftev2 = (sem(n) for n in ("s_ss", "s_rt", "s_fs", "s_ftr", "s_ftev", "s_ftev2"))
        s_sc, s_pr, s_lo, s_pv, s_oev = (sem(n) for n in ("s_sc", "s_pr", "s_lo", "s_pv", "s_oev"))
        (s_at, s_att, s_g, s_gsq, s_ss1, s_rn, s_gn, s_res, s_mean, s_cen, s_hsq, s_var, s_rstd, s_ln, s_hhi, s_hs,
         s_htr, s_htev, s_lg, s_lgr, s_exp, s_comb, s_ctr, s_cev, s_up, s_gelu, s_ex, s_hc, s_dn, s_yev, s_y, s_z,
         s_mean2, s_cen2, s_osq, s_var2, s_rstd2, s_fin, s_out) = (sem(n) for n in (
             "s_at", "s_att", "s_g", "s_gsq", "s_ss1", "s_rn", "s_gn", "s_res", "s_mean", "s_cen", "s_hsq", "s_var",
             "s_rstd", "s_ln", "s_hhi", "s_hs", "s_htr", "s_htev", "s_lg", "s_lgr", "s_exp", "s_comb", "s_ctr",
             "s_cev", "s_up", "s_gelu", "s_ex", "s_hc", "s_dn", "s_yev", "s_y", "s_z", "s_mean2", "s_cen2", "s_osq",
             "s_var2", "s_rstd2", "s_fin", "s_out"))
        s_ch = [sem(f"s_ch{i}") for i in range(6)]

        block = ctx.enter_context(nc.Block())

        def chained(eng, s, base=0):
            n = [0]

            def then(ins):
                n[0] += 1
                ins.then_inc(s, 1)
                eng.wait_ge(s, base + n[0])
            return then

        x_h = x.rearrange("b c (m h s) v -> b h c m (s v)", m=NM, h=2)
        out_t = out.rearrange("(bp b2) (v n) o -> bp b2 v n o", b2=2, n=NP)

        @block.sync
        def _(sp):
            for half in range(2):
                sp.dma_start(wraw[:, :, half, :], W.rearrange("o (g c) -> o g c", c=C)).then_inc(s_wg, 16)
            for b in range(B):
                for half in range(2):
                    if b >= XR:
                        sp.wait_ge(s_prod, b - XR + 1)
                    sp.dma_start(xring[64 * half:64 * half + 64, b % XR, :, :, :].rearrange("p m s v -> p m (s v)"),
                                 x_h[b, half]).then_inc(s_xb[b % XR], 16)
            for g in range(NG):
                sp.wait_ge(s_fin, g + 1)
                n0 = g * G % NP
                for b2 in range(2):
                    sp.dma_start(out_t[g * G // NP, b2, :, n0:n0 + G, :],
                                 h[64 * b2:64 * b2 + 64, g * G:(g + 1) * G, :]).then_inc(s_out, 16)
            sp.wait_ge(s_out, 16 * 2 * NG)

        @block.gpsimd
        def _(pool):
            pool.memset(wall[:, :], 0.0).then_inc(s_zero, 1)
            pool.wait_ge(s_zero, 1)
            for half in range(2):
                rows = slice(64 * half, 64 * half + 64)
                pool.dma_start(xedge[rows], x[:, :, T - 1, :].rearrange("b c v -> c b v")).then_inc(s_xe, 16)
                pool.dma_start(wall[rows, 0:512].rearrange("p (e k) -> p e k", e=E),
                               w1.rearrange("e d k -> d e k")).then_inc(s_w, 16)
                with nc.allow_non_contiguous_dma(reason="512 floats"):
                    pool.dma_start(wall[rows, 512:512 + E], router_w.rearrange("e d -> d e")).then_inc(s_w, 16)
                pool.dma_start(wall[half * E:half * E + E, 512 + E:], b2).then_inc(s_w, 16)
                pool.dma_start(w2s[rows], w2[half:E:2].rearrange("i k o -> k i o")).then_inc(s_w1r, 16)
                with nc.allow_non_contiguous_dma(reason="512 floats"):
                    pool.dma_start(b1s[rows], b1[half:E:2].rearrange("i k -> k i")).then_inc(s_w1r, 16)
            pool.wait_ge(s_cst, 16)
            nc.gpsimd.tensor_copy(ident16[:, :], ident).then_inc(s_id16, 1)
            nc.gpsimd.tensor_copy(sel[:, :], sel_f).then_inc(s_id16, 1)
            pool.wait_ge(s_w, 96)
            then = chained(pool, s_split)
            then(nc.gpsimd.tensor_copy(wp[:, 0, :], wall[:, :]))
            then(nc.gpsimd.tensor_tensor(wres[:, 0, :], wall[:, :], wp[:, 0, :], ALU.subtract))
            then(nc.gpsimd.tensor_copy(wp[:, 1, :], wres[:, 0, :]))
            then(nc.gpsimd.tensor_tensor(wres[:, 1, :], wres[:, 0, :], wp[:, 1, :], ALU.subtract))
            nc.gpsimd.tensor_copy(wp[:, 2, :], wres[:, 1, :]).then_inc(s_wp, 1)

            gt = nc.gpsimd.tensor_tensor

            def sl(n):
                return slice(n * G, n * G + G)

            def wide(v):
                return v.unsqueeze(2).to_broadcast([128, G, D])

            def rsqrt(dst, src, n):
                return gt(stat[:, dst, sl(n)], stat[:, src, sl(n)], minus_half, ALU.pow)

            def slot(g, s):
                x, y, z = g + 2, g + 1, g - 1
                if x < NG and s == 3:
                    pool.wait_ge(s_ss1, x + 1)
                    rsqrt(1, 0, x).then_inc(s_rn, 1)
                if x < NG and s == 5:
                    pool.wait_ge(s_gn, x + 1)
                    gt(h[:, sl(x), :], h[:, sl(x), :], f[:, sl(x), :], ALU.add).then_inc(s_res, 1)
                if x < NG and s == 7:
                    pool.wait_ge(s_mean, x + 1)
                    gt(h[:, sl(x), :], h[:, sl(x), :], wide(stat[:, 2, sl(x)]), ALU.subtract).then_inc(s_cen, 1)
                if 0 <= y < NG and s == 2:
                    pool.wait_ge(s_var, y + 1)
                    rsqrt(7, 3, y).then_inc(s_rstd, 1)
                if 0 <= y < NG and s == 4:
                    pool.wait_ge(s_hhi, y + 1)
                    gt(fs[:, sl(y), D:2 * D], h[:, sl(y), :], fs[:, sl(y), 0:D], ALU.subtract).then_inc(s_hs, 1)
                if 0 <= z < NG and s == 6:
                    pool.wait_ge(s_mean2, z + 1)
                    gt(h[:, sl(z), :], h[:, sl(z), :], wide(stat[:, 2, sl(z)]), ALU.subtract).then_inc(s_cen2, 1)
                if 1 <= z <= NG and s == 0:
                    pool.wait_ge(s_var2, z)
                    rsqrt(7, 3, z - 1).then_inc(s_rstd2, 1)

            for g in range(-2, NG + 3):
                for s in range(8):
                    slot(g, s)

        @block.tensor
        def _(pe):
            mm = nc.tensor.matmul
            pe.wait_ge(s_cst, 16)
            pe.wait_ge(s_wg, 32)
            for g in range(NF):
                last = mm(ps[:, D * g:D * g + D], wraw[:, g, :, :].rearrange("o h c -> o (h c)"), ident[0:D, 0:D],
                          is_transpose=True, start=True, stop=True)
            last.then_inc(s_wfold, 1)
            pe.wait_ge(s_weff, 1)

            def products(b):
                pe.wait_ge(s_xb[b % XR], 32 * (b // XR + 1))
                if b >= 2:
                    pe.wait_ge(s_prodev, b - 1)
                for q in range(2):
                    for s in range(HALF):
                        last = mm(bank(2 * (b % 2) + q).rearrange("p (m v) -> p m v", v=V), weff[:, s, :],
                                  xring[:, b % XR, 8 * q:8 * q + 8, s, :], start=(s == 0), stop=(s == HALF - 1))
                last.then_inc(s_prod, 1)

            def tokens(i):
                bp, n0 = i // 2, 8 * (i % 2)
                pe.wait_ge(s_prodev, 2 * bp + 2)
                if i == 0:
                    pe.wait_ge(s_padev, 1)
                if i >= 2:
                    pe.wait_ge(s_h, i - 1)
                for k in range(8):
                    for s in range(2):
                        last = mm(bank(4 + 2 * (i % 2) + s)[:, 64 * k:64 * k + 64],
                                  prod[64 * s:64 * s + 64, bp, n0 + k + s, :, :].rearrange("p c v -> p (c v)"),
                                  ident[64 * s:64 * s + 64, 64 * s:64 * s + 64], is_transpose=True, start=True, stop=True)
                last.then_inc(s_tr, 1)

            for b in range(B):
                products(b)
                if b == 1:
                    pe.wait_ge(s_xe, 32)
                    for s in range(HALF):
                        last = mm(bank(7).rearrange("p (b v) -> p b v", v=V), weff[:, s, :], xedge[:, :, :],
                                  start=(s == 0), stop=(s == HALF - 1))
                    last.then_inc(s_pad, 1)
                if b >= 2 and b % 2 == 0:
                    tokens(b - 2)
                    tokens(b - 1)
            for i in (B - 2, B - 1):
                tokens(i)
            pe.wait_ge(s_id16, 2)
            pe.wait_ge(s_prodev, B)
            for i in range(NT // 8):
                pe.wait_ge(s_fs, i // 2 + 1)
                if i == 1:
                    pe.wait_ge(s_h, 2 * BP)
                if i >= 2:
                    pe.wait_ge(s_ftev, i - 1)
                    pe.wait_ge(s_ftev2, 2 * (i - 1))
                for kind in range(3):
                    dst = bank(3 * (i % 2) + kind).bitcast(F16)
                    for k in range(8):
                        j = 8 * i + k
                        if kind == 0:
                            last = mm(dst[:, 128 * k:128 * k + 128], fs[:, j, :], ident16[:, :], is_transpose=True,
                                      start=True, stop=True)
                        else:
                            for rows in (0, 64):
                                last = mm(dst[rows:rows + 64, 128 * k:128 * k + 128],
                                          fs[:, j, 64 * (kind - 1):64 * kind], ident16[:, :], is_transpose=True,
                                          start=True, stop=True)
                last.then_inc(s_ftr, 1)

            def scores(k, q0):
                for half in range(2):
                    for i in (1, 2):
                        last = mm(bank(2 * (k % 2) + half), fT[0][:, 128 * k:128 * k + 128],
                                  fT[i][:, bass.ds(q0 + 512 * half, 512)], start=(i == 1), stop=(i == 2))
                last.then_inc(s_sc, 1)

            def weighted(t, first_probs):
                pe.wait_ge(s_pr, first_probs + 2 * t + 2)
                for e in range(2):
                    k = 2 * t + e
                    for half in range(2):
                        mm(bank(4 + half), fs[:, k, :],
                           probs[:, 2 * (t % 2) + e, :].bitcast(BF16)[:, 1024 * half + 1:1024 * half + 1024:2],
                           start=(k == 0), stop=False, skip_group_check=True)
                pe.wait_ge(s_lo, first_probs + 2 * t + 2)
                for half in range(2):
                    for e in range(2):
                        k = 2 * t + e
                        last = mm(bank(4 + half)[64 * e:64 * e + 64, :], fs[:, k, 0:64],
                                  probs_lo[:, 2 * (t % 2) + e, 512 * half:512 * half + 512],
                                  start=False, stop=(k >= NT - 2), skip_group_check=True)
                last.then_inc(s_pv, 1)
                return last

            pe.wait_ge(s_ftev, NT // 8)
            pe.wait_ge(s_ftev2, 2 * (NT // 8))
            scores(0, 0)
            scores(1, 0)

            def chunk(q, last_chunk):
                for t in range(PAIRS):
                    if t < PAIRS - 1 or not last_chunk:
                        nk, nq = (2 * t + 2, q * QC) if t < PAIRS - 1 else (0, (q + 1) * QC)
                        for e in range(2):
                            pe.wait_ge(s_pr, q * NT + 2 * t + 1 + e)
                            scores(nk + e, nq)
                    if t == 0 and not (isinstance(q, int) and q == 0):
                        pe.wait_ge(s_oev, q)
                    weighted(t, q * NT)

            chunk(0, False)
            with pe.Fori(1, NQ - 1) as q:
                chunk(q, False)
            chunk(NQ - 1, True)

            pe.wait_ge(s_oev, NQ)
            pe.wait_ge(s_wp, 1)
            pe.wait_ge(s_w1r, 64)

            def attention_tokens(x):
                if x >= 1:
                    pe.wait_ge(s_att, x)
                for k in range(G):
                    last = mm(bank(0)[:, D * k:D * k + D], outT[:, 128 * (G * x + k):128 * (G * x + k) + 128], both,
                              start=True, stop=True)
                last.then_inc(s_at, 1)

            def token_transposes(y):
                pe.wait_ge(s_hs, y + 1)
                if y >= 1:
                    pe.wait_ge(s_cev, y)
                for k in range(G):
                    last = mm(bank(1).bitcast(F16)[:, 128 * k:128 * k + 128], fs[:, G * y + k, :], ident16[:, :],
                              is_transpose=True, start=True, stop=True)
                last.then_inc(s_htr, 1)

            def router_logits(y):
                pe.wait_ge(s_htev, y + 1)
                for k in range(G):
                    for part in range(3):
                        last = mm(bank(1)[:, E * k:E * k + E], hT[:, 128 * (G * y + k):128 * (G * y + k) + 128],
                                  wp[:, part, 512:512 + E], start=(part == 0), stop=(part == 2))
                last.then_inc(s_lg, 1)

            def combine_transposes(y):
                pe.wait_ge(s_comb, y + 1)
                for k in range(G):
                    last = mm(bank(1).bitcast(F16)[0:2 * E, 128 * k:128 * k + 128], combine[:, y % 2, k, :],
                              ident16[:, :], is_transpose=True, start=True, stop=True)
                last.then_inc(s_ctr, 1)

            def up(u):
                n, i = u // NPAIR, u % NPAIR
                if u >= 2:
                    pe.wait_ge(s_gelu, u - 1)
                for part in range(3):
                    last = mm(bank(2 + u % 2), wp[:, part, 128 * i:128 * i + 128], hT[:, 512 * n:512 * n + 512],
                              start=(part == 0), stop=(part == 2))
                last.then_inc(s_up, 1)

            def expand(u):
                n, i = u // NPAIR, u % NPAIR
                pe.wait_ge(s_cev, n // NCH + 1)
                if u >= 2:
                    pe.wait_ge(s_hc, u - 1)
                t0 = 512 * (n % NCH)
                mm(bank(4 + u % 2), sel[:, 128 * i:128 * i + 128], combT[:, n // NCH % 2, t0:t0 + 512],
                   start=True, stop=True).then_inc(s_ex, 1)

            def down(u):
                n, i = u // NPAIR, u % NPAIR
                if i == 0 and n >= 1:
                    pe.wait_ge(s_yev, n)
                pe.wait_ge(s_hc, u + 2)
                for e in range(2):
                    last = mm(bank(6)[64 * e:64 * e + 64, :], w2s[:, i + e, :], hidc[:, (u + e) % 4, :],
                              start=(i == 0), stop=(i == 2), skip_group_check=True)
                last.then_inc(s_dn, 1)

            def result(n):
                pe.wait_ge(s_yev, n + 1)
                if n >= 1:
                    pe.wait_ge(s_z, n)
                for k in range(CH):
                    dst = bank(7)[:, D * k:D * k + D]
                    mm(dst, yT[:, n % 2, 128 * k:128 * k + 128], both, start=True, stop=False)
                    t0 = 512 * (n % NCH) + 128 * k
                    for part in range(3):
                        last = mm(dst, combT[:, n // NCH % 2, t0:t0 + 128], wp[0:2 * E, part, 512 + E:],
                                  start=False, stop=(part == 2))
                last.then_inc(s_y, 1)

            for g in range(-2, NG + 1):
                for s in range(8):
                    u = 8 * g + s
                    if s == 0 and g + 2 < NG:
                        attention_tokens(g + 2)
                    if s == 0 and 0 <= g < NG:
                        combine_transposes(g)
                    if 0 <= u < 8 * NG:
                        up(u)
                    if 1 <= u <= 8 * NG:
                        expand(u - 1)
                    if u >= 4 and u % 2 == 0 and u - 4 < 8 * NG:
                        down(u - 4)
                    if u >= 7 and u % 4 == 3 and (u - 7) // 4 < 2 * NG:
                        result((u - 7) // 4)
                    if s == 5 and 0 <= g + 1 < NG:
                        token_transposes(g + 1)
                    if s == 6 and 0 <= g + 1 < NG:
                        router_logits(g + 1)

        @block.scalar
        def _(act):
            a = nc.scalar.activation
            act.dma_start(cst[:, :], consts).then_inc(s_cst, 16)
            def root(g):
                act.wait_ge(s_ss, g + 1)
                a(stat[:, 1, HG * g:HG * g + HG], stat[:, 0, HG * g:HG * g + HG], ACT.Sqrt).then_inc(s_rt, 1)

            for b in range(B):
                act.wait_ge(s_prod, b + 1)
                a(prod[:, b // 2, 0:NM, b % 2, :], bank(2 * (b % 2), 2).rearrange("p (m v) -> p m v", v=V),
                  ACT.Copy).then_inc(s_prodev, 1)
                if b == 1:
                    act.wait_ge(s_pad, 1)
                    a(prod[:, :, NM, :, :], bank(7).rearrange("p (b c v) -> p b c v", c=2, v=V),
                      ACT.Copy).then_inc(s_padev, 1)
                if b >= 3 and b % 2:
                    root((b - 3) // 2)
            root(BP - 1)
            for i in range(NT // 8):
                act.wait_ge(s_ftr, i + 1)
                a(fT[2][:, 1024 * i:1024 * i + 1024], bank(3 * (i % 2) + 2).bitcast(F16)[:, 0:1024],
                  ACT.Copy).then_inc(s_ftev, 1)

            def exps(q, first):
                for k in range(NT):
                    act.wait_ge(s_sc, q * NT + k + 1)
                    if not (first and k < 4):
                        act.wait_ge(s_pv, q * PAIRS + k // 2 - 1)
                    a(probs[:, k % 4, :], bank(2 * (k % 2), 2), ACT.Exp,
                      accum_out=rowsum[:, bass.ds(q * NT + k, 1)]).then_inc(s_pr, 1)
            exps(0, True)
            with act.Fori(1, NQ) as q:
                exps(q, False)

            def sl(n):
                return slice(n * G, n * G + G)

            for g in range(-2, NG + 2):
                for s in range(8):
                    u, x, y, z = 8 * g + s, g + 2, g + 1, g - 1
                    if s == 0 and 0 <= g < NG:
                        act.wait_ge(s_ctr, g + 1)
                        if g >= 2:
                            act.wait_ge(s_y, 2 * g - 2)
                        a(combT[:, g % 2, :], bank(1).bitcast(F16)[0:2 * E, :], ACT.Copy).then_inc(s_cev, 1)
                    if 0 <= u < 8 * NG:
                        act.wait_ge(s_up, u + 1)
                        if u >= 4:
                            act.wait_ge(s_hc, u - 3)
                        a(hid[:, u % 4, :], bank(2 + u % 2), ACT.Gelu, bias=b1s[:, u % 4:u % 4 + 1]).then_inc(s_gelu, 1)
                    if u >= 6 and u % 4 == 2 and (u - 6) // 4 < 2 * NG:
                        n = (u - 6) // 4
                        act.wait_ge(s_dn, 2 * n + 2)
                        if n >= 2:
                            act.wait_ge(s_y, n - 1)
                        a(yT[:, n % 2, :], bank(6), ACT.Copy).then_inc(s_yev, 1)
                    if s == 1 and x < NG:
                        act.wait_ge(s_g, x + 1)
                        a(sq_g, f[:, sl(x), :], ACT.Square).then_inc(s_gsq, 1)
                    if s == 0 and 0 <= y < NG:
                        act.wait_ge(s_cen, y + 1)
                        a(sq_h, h[:, sl(y), :], ACT.Square).then_inc(s_hsq, 1)
                    if s == 3 and 0 <= y < NG:
                        act.wait_ge(s_ln, y + 1)
                        a(fs[:, sl(y), 0:D], h[:, sl(y), :], ACT.Copy).then_inc(s_hhi, 1)
                    if s == 5 and 0 <= y < NG:
                        act.wait_ge(s_htr, y + 1)
                        a(hT[:, 1024 * y:1024 * y + 1024], bank(1).bitcast(F16), ACT.Copy).then_inc(s_htev, 1)
                    if s == 6 and 0 <= y < NG:
                        act.wait_ge(s_lgr, y + 1)
                        a(rtmp[:, 1, :], rtmp[:, 0, :], ACT.Exp).then_inc(s_exp, 1)
                    if s == 7 and z >= 0 and z < NG:
                        act.wait_ge(s_cen2, z + 1)
                        a(sq_o, h[:, sl(z), :], ACT.Square).then_inc(s_osq, 1)

        @block.vector
        def _(dve):
            tt, ts, cp, red = nc.vector.tensor_tensor, nc.vector.tensor_scalar, nc.vector.tensor_copy, nc.vector.tensor_reduce
            stt = nc.vector.scalar_tensor_tensor

            def wide(v, n, d=D):
                return v.unsqueeze(2).to_broadcast([128, n, d])

            dve.wait_ge(s_wfold, 1)
            raw = ps[:, 0:NF * D].rearrange("p (g o) -> p g o", o=D)
            for s in range(HALF):
                tt(wdft[s], raw, wide(dft[:, s, :], NF), ALU.mult).then_inc(s_fold, 1)
            for s in range(HALF):
                dve.wait_ge(s_fold, s + 1)
                by_f = wdft[s].rearrange("p (r f) o -> p o r f", r=2)
                for odd in range(2):
                    last = red(wpar[:, odd, s, :], by_f[:, :, :, odd::2], AX.XY, ALU.add)
            last.then_inc(s_fold, 1)
            dve.wait_ge(s_fold, HALF + 1)
            tt(weff[:, :, 0:D], wpar[:, 0], wpar[:, 1], ALU.add)
            tt(weff[:, :, D:2 * D], wpar[:, 0], wpar[:, 1], ALU.subtract).then_inc(s_weff, 1)
            then = chained(dve, s_ch[0])
            for g in range(BP):
                sl = slice(g * HG, g * HG + HG)
                for i in (2 * g, 2 * g + 1):
                    dve.wait_ge(s_tr, i + 1)
                    red(h[:, 8 * i:8 * i + 8, :],
                        bank(4 + 2 * (i % 2), 2).rearrange("p (s n o) -> p n o s", s=2, o=D),
                        AX.X, ALU.add).then_inc(s_h, 1)
                dve.wait_ge(s_h, 2 * g + 2)
                then(tt(tmp[:, :, :], h[:, sl, :], h[:, sl, :], ALU.mult))
                red(stat[:, 0, sl], tmp[:, :, :], AX.X, ALU.add).then_inc(s_ss, 1)
                dve.wait_ge(s_rt, g + 1)
                then(ts(stat[:, 2, sl], stat[:, 1, sl], 1e-12, None, ALU.max))
                then(nc.vector.reciprocal(stat[:, 3, sl], stat[:, 2, sl]))
                then(tt(f[:, sl, :], h[:, sl, :], wide(stat[:, 3, sl], HG), ALU.mult))
                then(cp(fs[:, sl, 0:D], f[:, sl, :]))
                tt(fs[:, sl, D:2 * D], f[:, sl, :], fs[:, sl, 0:D], ALU.subtract).then_inc(s_fs, 1)
            dve.wait_ge(s_prodev, B)
            for i in range(NT // 8):
                dve.wait_ge(s_ftr, i + 1)
                for kind in range(2):
                    cp(fT[kind][:, 1024 * i:1024 * i + 1024],
                       bank(3 * (i % 2) + kind).bitcast(F16)[:, 0:1024]).then_inc(s_ftev2, 1)

            def low_parts(q, first):
                for k in range(NT):
                    dve.wait_ge(s_pr, q * NT + k + 1)
                    if not (first and k < 4):
                        dve.wait_ge(s_pv, q * PAIRS + k // 2 - 1)
                    tt(probs_lo[:, k % 4, :], probs[:, k % 4, :], probs[:, k % 4, :].bitcast(BF16)[:, 1:2 * QC:2],
                       ALU.subtract).then_inc(s_lo, 1)
                    if k == 0 and not first:
                        sums_out(q - 1)

            def sums_out(q):
                dve.wait_ge(s_pv, (q + 1) * PAIRS)
                cp(outT[:, bass.ds(q * QC, QC)], bank(4, 2)).then_inc(s_oev, 1)

            low_parts(0, True)
            with dve.Fori(1, NQ) as q:
                low_parts(q, False)
            sums_out(NQ - 1)

            then = chained(dve, s_ch[1])
            dve.wait_ge(s_pr, NQ * NT)
            then(red(stat[:, 4, :], rowsum[:, :].rearrange("p (q k) -> p k q", q=NQ), AX.X, ALU.add))
            then(nc.vector.reciprocal(stat[:, 5, :], stat[:, 4, :]))
            then(ts(stat[:, 6, :], stat[:, 5, :], 1.0 - 0.8, None, ALU.mult))

            def sl(n):
                return slice(n * G, n * G + G)

            def attended(x):
                dve.wait_ge(s_at, x + 1)
                att_t = att.rearrange("p (j o) -> p j o", o=D)
                tt(att_t, bank(0).rearrange("p (j o) -> p j o", o=D), wide(stat[:, 6, sl(x)], G),
                   ALU.mult).then_inc(s_att, 1)
                dve.wait_ge(s_att, x + 1)
                stt(f[:, sl(x), :], f[:, sl(x), :], 0.8, att_t, ALU.mult, ALU.add).then_inc(s_g, 1)

            def attended_squares(x):
                dve.wait_ge(s_gsq, x + 1)
                then(red(stat[:, 5, sl(x)], sq_g, AX.X, ALU.add))
                ts(stat[:, 0, sl(x)], stat[:, 5, sl(x)], 1e-24, None, ALU.max).then_inc(s_ss1, 1)

            def attended_normed(x):
                dve.wait_ge(s_rn, x + 1)
                tt(f[:, sl(x), :], f[:, sl(x), :], wide(stat[:, 1, sl(x)], G), ALU.mult).then_inc(s_gn, 1)

            def mean(n, ready, done):
                dve.wait_ge(*ready)
                then(red(stat[:, 5, sl(n)], h[:, sl(n), :], AX.X, ALU.add))
                ts(stat[:, 2, sl(n)], stat[:, 5, sl(n)], 1.0 / D, None, ALU.mult).then_inc(done, 1)

            def variance(n, squares, ready, done):
                dve.wait_ge(*ready)
                then(red(stat[:, 5, sl(n)], squares, AX.X, ALU.add))
                ts(stat[:, 3, sl(n)], stat[:, 5, sl(n)], 1.0 / D, 1e-5, ALU.mult, ALU.add).then_inc(done, 1)

            def scaled(n, ready, done):
                dve.wait_ge(*ready)
                tt(h[:, sl(n), :], h[:, sl(n), :], wide(stat[:, 7, sl(n)], G), ALU.mult).then_inc(done, 1)

            def by_tile(v):
                return v.rearrange("p (t e) -> p t e", e=E)

            def R(i):
                return by_tile(rtmp[:, i, :])

            def per_tile(i):
                return rtmp[:, 11, G * i:G * i + G]

            def of_tile(i):
                return wide(per_tile(i), G, E)

            numbers = enum.unsqueeze(1).to_broadcast([128, G, E])

            def routing(y, part):
                if part == 0:
                    dve.wait_ge(s_lg, y + 1)
                    logits = by_tile(bank(1)[:, 0:G * E])
                    then(red(per_tile(0), logits, AX.X, ALU.max))
                    tt(R(0), logits, of_tile(0), ALU.subtract).then_inc(s_lgr, 1)
                    dve.wait_ge(s_lgr, y + 1)
                    then(stt(R(2), R(0), 0.0, numbers, ALU.is_equal, ALU.mult))
                    then(red(per_tile(1), R(2), AX.X, ALU.min))
                    then(tt(R(3), numbers, of_tile(1), ALU.is_equal))
                    then(stt(R(4), R(3), -1e30, R(0), ALU.mult, ALU.add))
                    then(red(per_tile(2), R(4), AX.X, ALU.max))
                if part == 1:
                    then(tt(R(5), R(4), of_tile(2), ALU.is_equal))
                    then(tt(R(6), R(5), numbers, ALU.mult))
                    then(red(per_tile(3), R(6), AX.X, ALU.min))
                    then(tt(R(7), numbers, of_tile(3), ALU.is_equal))
                    then(tt(R(8), R(3), R(7), ALU.add))
                    dve.wait_ge(s_exp, y + 1)
                    red(per_tile(4), R(1), AX.X, ALU.add)
                    then(tt(R(9), R(8), R(1), ALU.mult))
                    then(red(per_tile(5), R(9), AX.X, ALU.add))
                if part == 2:
                    then(stt(per_tile(6), per_tile(4), 1e-12, per_tile(5), ALU.mult, ALU.max))
                    then(nc.vector.reciprocal(per_tile(7), per_tile(6)))
                    then(tt(R(10), R(9), of_tile(7), ALU.mult))
                    if y >= 2:
                        dve.wait_ge(s_ctr, y - 1)
                    then(cp(combine[:, y % 2, :, 0:E], R(10)))
                    tt(combine[:, y % 2, :, E:2 * E], R(10), combine[:, y % 2, :, 0:E], ALU.subtract).then_inc(s_comb, 1)

            def weigh(u):
                dve.wait_ge(s_gelu, u + 1)
                dve.wait_ge(s_ex, u + 1)
                if u >= 4:
                    dve.wait_ge(s_dn, u // 2 - 1)
                tt(hidc[:, u % 4, :], hid[:, u % 4, :], bank(4 + u % 2), ALU.mult).then_inc(s_hc, 1)

            def residual(n):
                dve.wait_ge(s_y, n + 1)
                t = slice(CH * n, CH * n + CH)
                stt(h[:, t, :], h[:, t, :], 2.0, bank(7)[:, 0:CH * D].rearrange("p (j o) -> p j o", o=D),
                    ALU.mult, ALU.add).then_inc(s_z, 1)

            for g in range(-2, NG + 3):
                for s in range(8):
                    u, x, y, z = 8 * g + s, g + 2, g + 1, g - 1
                    if 1 <= u <= 8 * NG:
                        weigh(u - 1)
                    if u >= 8 and u % 4 == 0 and (u - 8) // 4 < 2 * NG:
                        residual((u - 8) // 4)
                    if s == 0 and x < NG:
                        attended(x)
                    if s == 2 and x < NG:
                        attended_squares(x)
                    if s == 4 and x < NG:
                        attended_normed(x)
                    if s == 6 and x < NG:
                        mean(x, (s_res, x + 1), s_mean)
                    if s == 1 and 0 <= y < NG:
                        variance(y, sq_h, (s_hsq, y + 1), s_var)
                    if s == 3 and 0 <= y < NG:
                        scaled(y, (s_rstd, y + 1), s_ln)
                    if s == 6 and 0 <= y < NG:
                        routing(y, 0)
                    if s == 7 and 0 <= y < NG:
                        routing(y, 1)
                        routing(y, 2)
                    if s == 5 and 0 <= z < NG:
                        mean(z, (s_z, 2 * z + 2), s_mean2)
                    if s == 7 and 0 <= z < NG:
                        variance(z, sq_o, (s_osq, z + 1), s_var2)
                    if s == 1 and 0 <= z - 1 < NG:
                        scaled(z - 1, (s_rstd2, z), s_fin)


_INS = ["x", "L0_tok_W", "L0_ffn_router_w", "L0_ffn_w1", "L0_ffn_b1", "L0_ffn_w2", "L0_ffn_b2"]


def kernel(**inputs):
    import numpy as _np
    import concourse.bacc as _bacc
    from concourse import mybir as _mybir
    from concourse.bass_utils import run_bass_kernel_spmd as _run

    nc = _bacc.Bacc("TRN2", target_bir_lowering=False, num_devices=1)
    arrays, args = {}, []
    for name in _INS:
        a = _np.ascontiguousarray(inputs[name])
        arrays[f"in_{name}_dram"] = a
        args.append(nc.dram_tensor(f"in_{name}_dram", a.shape, _mybir.dt.from_np(a.dtype), kind="ExternalInput").ap())
    c = constants()
    arrays["consts_dram"] = c
    args.append(nc.dram_tensor("consts_dram", c.shape, _mybir.dt.from_np(c.dtype), kind="ExternalInput").ap())
    args.append(nc.dram_tensor("out_dram", (B, V * NP, D), _mybir.dt.float32, kind="ExternalOutput").ap())
    tower(nc, *args)
    r = _run(nc, [arrays], core_ids=[0])
    return r.results[0]["out_dram"]
```

```python
import math
from contextlib import ExitStack

import numpy as np

import concourse.bass as bass
from concourse import mybir

F32 = mybir.dt.float32
F16 = mybir.dt.float16
BF16 = mybir.dt.bfloat16
ALU = mybir.AluOpType
ACT = mybir.ActivationFunctionType
AX = mybir.AxisListType

B, C, T, V = 8, 64, 128, 64
PATCH, STRIDE = 16, 8
NP = (T + STRIDE - PATCH) // STRIDE + 1
NM = T // STRIDE
NF = 2 * (PATCH // 2 + 1)
D = 64
E = 8
HALF = STRIDE // 2
BP = B // 2
NT = BP * NP
NTOK = 128 * NT
QC = 1024
NQ = NTOK // QC
PAIRS = NT // 2
START = (3, 8, 13)
EARLY = len(START)
LATE_SPLITS = {2: 5, 6: 6, 10: 7}
NPAIR = E // 2
G = 8
NG = NT // G
CH = 4
NCH = G // CH
WIDE = NPAIR * 128 + E + D
XR = 3
XLEN = NM * HALF * V
CONSTS = 128 + HALF * NF + E + D + 2 * G


def constants():
    c = np.zeros((128, CONSTS + NPAIR * 128), np.float32)
    c[:, 0:128] = np.eye(128)
    for half in range(2):
        for s in range(HALF):
            for f in range(PATCH // 2 + 1):
                a = 2 * math.pi * f * (HALF * half + s) / PATCH
                c[64 * half:64 * half + 64, 128 + NF * s + f] = math.cos(a) / math.sqrt(PATCH)
                c[64 * half:64 * half + 64, 128 + NF * s + NF // 2 + f] = -math.sin(a) / math.sqrt(PATCH)
    at = 128 + HALF * NF
    c[:, at:at + E] = np.arange(E) - E
    at += E
    for row in range(128):
        c[row, at + row % 64] = 1.0
    at += D
    c[:, at:at + G] = -0.5
    c[:, at + G:at + 2 * G] = math.e
    for e in range(E):
        for part in range(2):
            c[part * E + e, CONSTS + 64 * e:CONSTS + 64 * e + 64] = 1.0
    return c


def tower(nc, x, W, router_w, w1, b1, w2, b2, consts, out):
    ctx = ExitStack()
    with ctx:
        def sb(name, shape, dt):
            return ctx.enter_context(nc.sbuf_tensor(name, shape, dt))

        def sem(name):
            return ctx.enter_context(nc.semaphore(name))

        cst = sb("cst", [128, CONSTS], F32)
        ident = cst[:, 0:128]
        dft = cst[:, 128:128 + HALF * NF].rearrange("p (s g) -> p s g", s=HALF)
        at = 128 + HALF * NF
        enum = cst[:, at:at + E]
        at += E
        both = cst[:, at:at + D]
        minus_half = cst[:, at + D:at + D + G]
        euler = cst[:, at + D + G:at + D + 2 * G]
        ident16 = sb("ident16", [128, 128], F16)
        sel = sb("sel", [2 * E, NPAIR * 128], F16)
        weff = sb("weff", [128, HALF, 128], F32)
        xedge = sb("xedge", [128, B, V], F32)

        ring = sb("ring", [128, XR * XLEN], F32)
        xring = ring[:, :].rearrange("p (r m s v) -> p r m s v", r=XR, m=NM, s=HALF)
        probs = ring[:, 0:4 * QC].rearrange("p (i q) -> p i q", i=4)
        probs_lo = ring[:, 4 * QC:6 * QC].bitcast(F16).rearrange("p (i q) -> p i q", i=4)

        sums = sb("sums", [128, B * (NM + 1) * V], F32)
        prod = sums[:, :].rearrange("p (b m c v) -> p b m c v", b=BP, m=NM + 1, c=2)
        outT = sums[:, 0:NTOK]
        wres = sums[:, (NQ - 1) * QC:(NQ - 1) * QC + 2 * WIDE].rearrange("p (i k) -> p i k", i=2)
        big = sb("big", [128, 3 * NTOK // 2], F32)
        fT = [big[:, i * NTOK // 2:(i + 1) * NTOK // 2].bitcast(F16) for i in range(3)]
        h = sb("h", [128, NT, D], F32)
        f = sb("f", [128, NT, D], F32)
        wraw = f[0:D, 0:2 * NF, :].rearrange("o (g h) c -> o g h c", h=2)
        wdft = [h[:, NF * s:NF * s + NF, :] for s in range(3)] + [f[:, 2 * NF:3 * NF, :]]
        wpar = f[:, 3 * NF:3 * NF + 2 * HALF, :].rearrange("p (i s) o -> p i s o", i=2)
        fs = sb("fs", [128, NT, 2 * D], F16)
        sel_f = fs[0:2 * E, 0:2 * NPAIR * 128 // (2 * D), :].rearrange("p j o -> p (j o)").bitcast(F32)
        squares = sb("squares", [128, 2, G, D], F32)
        wpad = sb("wpad", [128, 128], F32)
        stat = sb("stat", [128, 8, NT], F32)
        rowsum = sb("rowsum", [128, NQ * NT], F32)
        rtmp = sb("rtmp", [128, 12, G * E], F32)
        rsmall = sb("rsmall", [128, 8, G], F32)
        wall = sb("wall", [128, WIDE], F32)
        wp = sb("wp", [128, 3, WIDE], BF16)
        w2s = sb("w2s", [128, NPAIR, D], F32)
        b1s = sb("b1s", [128, NPAIR], F32)
        hT = fT[0]
        combT = sb("combT", [2 * E, 2, G * 128], F16)
        late = ring[:, 0:15 * 512].rearrange("p (i t) -> p i t", t=512)
        hid, hidc, yT = late[:, 0:4], late[:, 4:8], late[:, 8:10]
        sq_o = late[:, 13, :].rearrange("p (j o) -> p j o", o=D)
        att, sq_g, sq_h = wall[:, 0:G * D].rearrange("p (j o) -> p j o", o=D), squares[:, 0], squares[:, 1]
        combine = late[:, 14, :].bitcast(F16)[:, 0:2 * G * 2 * E].rearrange("p (i j e) -> p i j e", i=2, e=2 * E)

        ps = ctx.enter_context(nc.psum_tensor("ps", [128, 4096], F32))

        def bank(i, n=1):
            return ps[:, 512 * i:512 * (i + n)]

        s_cst, s_self, s_wg, s_xe, s_w, s_w1r = (sem(n) for n in ("s_cst", "s_self", "s_wg", "s_xe", "s_w", "s_w1r"))
        s_xb = [sem(f"s_x{i}") for i in range(XR)]
        s_id16, s_zero, s_split, s_wp = (sem(n) for n in ("s_id16", "s_zero", "s_split", "s_wp"))
        s_wfold, s_weff, s_fold, s_sqf, s_wpad = (sem(n) for n in ("s_wfold", "s_weff", "s_fold", "s_sqf", "s_wpad"))
        s_prod, s_prodev, s_tr, s_h, s_pad, s_padev = (sem(n) for n in ("s_prod", "s_prodev", "s_tr", "s_h", "s_pad", "s_padev"))
        s_ss, s_rt, s_fs, s_ftr, s_ftev, s_ftev2 = (sem(n) for n in ("s_ss", "s_rt", "s_fs", "s_ftr", "s_ftev", "s_ftev2"))
        s_sc, s_pr, s_lo, s_pv, s_oev = (sem(n) for n in ("s_sc", "s_pr", "s_lo", "s_pv", "s_oev"))
        (s_at, s_att, s_g, s_gsq, s_ss1, s_rn, s_gn, s_res, s_mean, s_cen, s_hsq, s_var, s_rstd, s_ln, s_hhi, s_hs,
         s_htr, s_htev, s_lg, s_gap, s_route, s_centred, s_exp, s_comb, s_ctr, s_cev, s_up, s_gelu, s_ex, s_hc, s_dn, s_yev, s_y, s_z,
         s_mean2, s_cen2, s_osq, s_var2, s_rstd2, s_fin, s_out) = (sem(n) for n in (
             "s_at", "s_att", "s_g", "s_gsq", "s_ss1", "s_rn", "s_gn", "s_res", "s_mean", "s_cen", "s_hsq", "s_var",
             "s_rstd", "s_ln", "s_hhi", "s_hs", "s_htr", "s_htev", "s_lg", "s_gap", "s_route", "s_centred", "s_exp", "s_comb", "s_ctr",
             "s_cev", "s_up", "s_gelu", "s_ex", "s_hc", "s_dn", "s_yev", "s_y", "s_z", "s_mean2", "s_cen2", "s_osq",
             "s_var2", "s_rstd2", "s_fin", "s_out"))
        s_ch = [sem(f"s_ch{i}") for i in range(2)]

        block = ctx.enter_context(nc.Block())

        def chained(eng, s, base=0):
            n = [0]

            def then(ins):
                n[0] += 1
                ins.then_inc(s, 1)
                eng.wait_ge(s, base + n[0])
            return then

        x_h = x.rearrange("b c (m h s) v -> b h c m (s v)", m=NM, h=2)
        out_t = out.rearrange("(bp b2) (v n) o -> bp b2 v n o", b2=2, n=NP)

        @block.sync
        def _(sp):
            for half in range(2):
                sp.dma_start(wraw[:, :, half, :], W.rearrange("o (g c) -> o g c", c=C)).then_inc(s_wg, 16)
            for b in range(B):
                for half in range(2):
                    if b >= XR:
                        sp.wait_ge(s_prod, b - XR + 1)
                    sp.dma_start(xring[64 * half:64 * half + 64, b % XR, :, :, :].rearrange("p m s v -> p m (s v)"),
                                 x_h[b, half]).then_inc(s_xb[b % XR], 16)
            for g in range(NG):
                sp.wait_ge(s_fin, g + 1)
                n0 = g * G % NP
                for b2 in range(2):
                    sp.dma_start(out_t[g * G // NP, b2, :, n0:n0 + G, :],
                                 h[64 * b2:64 * b2 + 64, g * G:(g + 1) * G, :]).then_inc(s_out, 16)
            sp.wait_ge(s_out, 16 * 2 * NG)

        @block.gpsimd
        def _(pool):
            pool.memset(wall[:, :], 0.0).then_inc(s_zero, 1)
            pool.wait_ge(s_zero, 1)
            for half in range(2):
                rows = slice(64 * half, 64 * half + 64)
                pool.dma_start(xedge[rows], x[:, :, T - 1, :].rearrange("b c v -> c b v")).then_inc(s_xe, 16)
                pool.dma_start(wall[rows, 0:512].rearrange("p (e k) -> p e k", e=E),
                               w1.rearrange("e d k -> d e k")).then_inc(s_w, 16)
                with nc.allow_non_contiguous_dma(reason="512 floats"):
                    pool.dma_start(wall[rows, 512:512 + E], router_w.rearrange("e d -> d e")).then_inc(s_w, 16)
                pool.dma_start(wall[half * E:half * E + E, 512 + E:], b2).then_inc(s_w, 16)
                pool.dma_start(w2s[rows], w2[half:E:2].rearrange("i k o -> k i o")).then_inc(s_w1r, 16)
                with nc.allow_non_contiguous_dma(reason="512 floats"):
                    pool.dma_start(b1s[rows], b1[half:E:2].rearrange("i k -> k i")).then_inc(s_w1r, 16)
            pool.wait_ge(s_cst, 16)
            nc.gpsimd.tensor_copy(ident16[:, :], ident).then_inc(s_id16, 1)
            pool.wait_ge(s_self, 16)
            nc.gpsimd.tensor_copy(sel[:, :], sel_f).then_inc(s_id16, 1)
            gt = nc.gpsimd.tensor_tensor

            def sl(n):
                return slice(n * G, n * G + G)

            for i in range(NG):
                pool.wait_ge(s_ss, i + 1)
                gt(stat[:, 2, sl(i)], stat[:, 1, sl(i)], minus_half, ALU.pow).then_inc(s_rt, 1)
            pool.wait_ge(s_w, 96)
            then = chained(pool, s_split)
            then(nc.gpsimd.tensor_copy(wp[:, 0, :], wall[:, :]))
            then(gt(wres[:, 0, :], wall[:, :], wp[:, 0, :], ALU.subtract))
            then(nc.gpsimd.tensor_copy(wp[:, 1, :], wres[:, 0, :]))
            then(gt(wres[:, 1, :], wres[:, 0, :], wp[:, 1, :], ALU.subtract))
            nc.gpsimd.tensor_copy(wp[:, 2, :], wres[:, 1, :]).then_inc(s_wp, 1)

            def wide(v):
                return v.unsqueeze(2).to_broadcast([128, G, D])

            def rsqrt(dst, src, n):
                return gt(stat[:, dst, sl(n)], stat[:, src, sl(n)], minus_half, ALU.pow)

            def exponential(q):
                pool.wait_ge(s_gap, q + 1)
                gt(rsmall[:, 3, :], euler, rsmall[:, 2, :], ALU.pow).then_inc(s_exp, 1)

            def centre(y):
                pool.wait_ge(s_mean, y + 1)
                gt(h[:, sl(y), :], h[:, sl(y), :], wide(stat[:, 2, sl(y)]), ALU.subtract).then_inc(s_cen, 1)

            def attention_scale(x):
                pool.wait_ge(s_ss1, x + 1)
                rsqrt(1, 0, x).then_inc(s_rn, 1)

            def residual(x):
                pool.wait_ge(s_gn, x + 1)
                gt(h[:, sl(x), :], h[:, sl(x), :], f[:, sl(x), :], ALU.add).then_inc(s_res, 1)

            def deviation(y):
                pool.wait_ge(s_var, y + 1)
                rsqrt(7, 3, y).then_inc(s_rstd, 1)

            def low_half(y):
                pool.wait_ge(s_hhi, y + 1)
                gt(fs[:, sl(y), D:2 * D], h[:, sl(y), :], fs[:, sl(y), 0:D], ALU.subtract).then_inc(s_hs, 1)

            for t in range(PAIRS):
                for i in range(EARLY):
                    at = t - START[i]
                    if at == 4:
                        attention_scale(i)
                        pool.wait_ge(s_rn, i + 1)
                        gt(f[:, sl(i), :], f[:, sl(i), :], wide(stat[:, 1, sl(i)]), ALU.mult).then_inc(s_gn, 1)
                        residual(i)
                    if at == 6 and i < EARLY - 1:
                        centre(i)
                    if at == 9 and i < EARLY - 1:
                        deviation(i)
                        pool.wait_ge(s_rstd, i + 1)
                        gt(h[:, sl(i), :], h[:, sl(i), :], wide(stat[:, 7, sl(i)]), ALU.mult).then_inc(s_ln, 1)
                    if at == 12 and i < EARLY - 1:
                        low_half(i)
                    if at == 19 and i == 0:
                        exponential(0)

            def elementwise(x, y, q, z):
                if y < NG:
                    centre(y)
                if z >= 1:
                    pool.wait_ge(s_var2, z)
                    rsqrt(7, 3, z - 1).then_inc(s_rstd2, 1)
                if x < NG:
                    attention_scale(x)
                if y < NG:
                    deviation(y)
                if q < NG:
                    exponential(q)
                if y < NG:
                    low_half(y)
                if x < NG:
                    residual(x)
                if z >= 1:
                    pool.wait_ge(s_rstd2, z)
                    gt(h[:, sl(z - 1), :], h[:, sl(z - 1), :], wide(stat[:, 7, sl(z - 1)]), ALU.mult).then_inc(s_fin, 1)
                if 0 <= z < NG:
                    pool.wait_ge(s_mean2, z + 1)
                    gt(h[:, sl(z), :], h[:, sl(z), :], wide(stat[:, 2, sl(z)]), ALU.subtract).then_inc(s_cen2, 1)

            for g in range(0, NG + 2):
                elementwise(g + 3, g + 2, g + 1, g - 1)

        @block.tensor
        def _(pe):
            mm = nc.tensor.matmul
            pe.wait_ge(s_cst, 16)
            pe.wait_ge(s_wg, 32)
            for g in range(NF):
                last = mm(ps[:, D * g:D * g + D], wraw[:, g, :, :].rearrange("o h c -> o (h c)"), ident[0:D, 0:D],
                          is_transpose=True, start=True, stop=True)
            last.then_inc(s_wfold, 1)
            pe.wait_ge(s_weff, 1)

            def products(b):
                pe.wait_ge(s_xb[b % XR], 32 * (b // XR + 1))
                if b >= 2:
                    pe.wait_ge(s_prodev, b - 1)
                for q in range(2):
                    for s in range(HALF):
                        last = mm(bank(2 * (b % 2) + q).rearrange("p (m v) -> p m v", v=V), weff[:, s, :],
                                  xring[:, b % XR, 8 * q:8 * q + 8, s, :], start=(s == 0), stop=(s == HALF - 1))
                last.then_inc(s_prod, 1)

            def tokens(i):
                bp, n0 = i // 2, 8 * (i % 2)
                pe.wait_ge(s_prodev, 2 * bp + 2)
                pe.wait_ge(s_padev, 1)
                if i >= 1:
                    pe.wait_ge(s_h, i)
                for k in range(8):
                    for s in range(2):
                        last = mm(bank(4 + s)[:, 64 * k:64 * k + 64],
                                  prod[64 * s:64 * s + 64, bp, n0 + k + s, :, :].rearrange("p c v -> p (c v)"),
                                  ident[64 * s:64 * s + 64, 64 * s:64 * s + 64], is_transpose=True, start=True, stop=True)
                last.then_inc(s_tr, 1)

            def split_transposes(i):
                pe.wait_ge(s_fs, i + 1)
                for kind in range(3):
                    n = 3 * i + kind
                    if n >= 2:
                        before = n - 2
                        pe.wait_ge(*((s_ftev, before // 3 + 1) if before % 3 == 2 else
                                     (s_ftev2, 2 * (before // 3) + before % 3 + 1)))
                    dst = bank(6 + n % 2).bitcast(F16)
                    for k in range(8):
                        j = 8 * i + k
                        if kind == 0:
                            last = mm(dst[:, 128 * k:128 * k + 128], fs[:, j, :], ident16[:, :], is_transpose=True,
                                      start=True, stop=True)
                        else:
                            for rows in (0, 64):
                                last = mm(dst[rows:rows + 64, 128 * k:128 * k + 128],
                                          fs[:, j, 64 * (kind - 1):64 * kind], ident16[:, :], is_transpose=True,
                                          start=True, stop=True)
                    last.then_inc(s_ftr, 1)

            for b in range(B):
                products(b)
                if b == 1:
                    pe.wait_ge(s_xe, 32)
                    pe.wait_ge(s_wpad, 1)
                    mm(bank(7).rearrange("p (b v) -> p b v", v=V), wpad[:, :], xedge[:, :, :],
                       start=True, stop=True).then_inc(s_pad, 1)
                if b >= 2:
                    tokens(b - 2)
                if b >= 4:
                    if b == 4:
                        pe.wait_ge(s_id16, 2)
                    split_transposes(b - 4)
            tokens(B - 2)
            split_transposes(4)
            tokens(B - 1)

            def scores(k, q0):
                for half in range(2):
                    for i in (1, 2):
                        last = mm(bank(2 * (k % 2) + half), fT[0][:, 128 * k:128 * k + 128],
                                  fT[i][:, bass.ds(q0 + 512 * half, 512)], start=(i == 1), stop=(i == 2))
                last.then_inc(s_sc, 1)

            def weighted(t, first_probs):
                pe.wait_ge(s_pr, first_probs + 2 * t + 2)
                for e in range(2):
                    k = 2 * t + e
                    for half in range(2):
                        mm(bank(4 + half), fs[:, k, :],
                           probs[:, 2 * (t % 2) + e, :].bitcast(BF16)[:, 1024 * half + 1:1024 * half + 1024:2],
                           start=(k == 0), stop=False, skip_group_check=True)
                pe.wait_ge(s_lo, first_probs + 2 * t + 2)
                for half in range(2):
                    for e in range(2):
                        k = 2 * t + e
                        last = mm(bank(4 + half)[64 * e:64 * e + 64, :], fs[:, k, 0:64],
                                  probs_lo[:, 2 * (t % 2) + e, 512 * half:512 * half + 512],
                                  start=False, stop=(k >= NT - 2), skip_group_check=True)
                last.then_inc(s_pv, 1)
                return last

            pe.wait_ge(s_prodev, B)
            pe.wait_ge(s_ftev, 1)
            pe.wait_ge(s_ftev2, 2)
            scores(0, 0)
            scores(1, 0)

            def attention_tokens(x, k0=0, k1=G):
                if x >= 1 and k0 == 0:
                    pe.wait_ge(s_att, x)
                for k in range(k0, k1):
                    last = mm(bank(6)[:, D * k:D * k + D], outT[:, 128 * (G * x + k):128 * (G * x + k) + 128], both,
                              start=True, stop=True)
                if k1 == G:
                    last.then_inc(s_at, 1)

            def token_transposes(y):
                pe.wait_ge(s_hs, y + 1)
                if y >= 1:
                    pe.wait_ge(s_centred, y)
                if y >= 2:
                    pe.wait_ge(s_cev, y - 1)
                for k in range(G):
                    last = mm(bank(7).bitcast(F16)[:, 128 * k:128 * k + 128], fs[:, G * y + k, :], ident16[:, :],
                              is_transpose=True, start=True, stop=True)
                last.then_inc(s_htr, 1)

            def router_logits(y):
                pe.wait_ge(s_wp, 1)
                pe.wait_ge(s_htev, y + 1)
                if y >= 1:
                    pe.wait_ge(s_cev, y)
                for k in range(G):
                    for part in range(3):
                        last = mm(bank(7)[:, E * k:E * k + E], hT[:, 128 * (G * y + k):128 * (G * y + k) + 128],
                                  wp[:, part, 512:512 + E], start=(part == 0), stop=(part == 2))
                last.then_inc(s_lg, 1)

            def combine_transposes(y):
                pe.wait_ge(s_comb, y + 1)
                pe.wait_ge(s_htev, min(y + 2, NG))
                for k in range(G):
                    last = mm(bank(7).bitcast(F16)[0:2 * E, 128 * k:128 * k + 128], combine[:, y % 2, k, :],
                              ident16[:, :], is_transpose=True, start=True, stop=True)
                last.then_inc(s_ctr, 1)

            def up(u):
                n, i = u // NPAIR, u % NPAIR
                if u >= 2:
                    pe.wait_ge(s_gelu, u - 1)
                for part in range(3):
                    last = mm(bank(u % 2), wp[:, part, 128 * i:128 * i + 128], hT[:, 512 * n:512 * n + 512],
                              start=(part == 0), stop=(part == 2))
                last.then_inc(s_up, 1)

            def beside(t):
                for i in range(EARLY):
                    at = t - START[i]
                    if at == -1:
                        attention_tokens(i)
                    if at == 12 and i == EARLY - 1:
                        attention_tokens(i + 1)
                    if at == 15 and i < EARLY - 1:
                        token_transposes(i)
                    if at == 17 and i == 0:
                        router_logits(i)
                    if at == 25 and i == 0:
                        combine_transposes(i)
                if t == PAIRS - 1:
                    pe.wait_ge(s_pr, NQ * NT - 1)
                    up(0)
                    up(1)

            def chunk(q, last_chunk):
                first = isinstance(q, int) and q == 0
                for t in range(PAIRS):
                    if last_chunk:
                        beside(t)
                    if first and t in LATE_SPLITS:
                        split_transposes(LATE_SPLITS[t])
                    if first and t % 4 == 3 and t < PAIRS - 1:
                        pe.wait_ge(s_ftev, (t + 1) // 4 + 1)
                        pe.wait_ge(s_ftev2, 2 * ((t + 1) // 4) + 2)
                    if first and t == 0:
                        pe.wait_ge(s_h, NG)
                    if t < PAIRS - 1 or not last_chunk:
                        nk, nq = (2 * t + 2, q * QC) if t < PAIRS - 1 else (0, (q + 1) * QC)
                        for e in range(2):
                            pe.wait_ge(s_pr, q * NT + 2 * t + 1 + e)
                            scores(nk + e, nq)
                    if t == 0 and not (isinstance(q, int) and q == 0):
                        pe.wait_ge(s_oev, q)
                    weighted(t, q * NT)

            chunk(0, False)
            with pe.Fori(1, NQ - 1) as q:
                chunk(q, False)
            chunk(NQ - 1, True)

            pe.wait_ge(s_w1r, 64)
            def expand(u):
                n, i = u // NPAIR, u % NPAIR
                pe.wait_ge(s_cev, n // NCH + 1)
                if u >= 2:
                    pe.wait_ge(s_hc, u - 1)
                t0 = 512 * (n % NCH)
                mm(bank(2 + u % 2), sel[:, 128 * i:128 * i + 128], combT[:, n // NCH % 2, t0:t0 + 512],
                   start=True, stop=True).then_inc(s_ex, 1)

            def down(u):
                n, i = u // NPAIR, u % NPAIR
                if u == 0:
                    pe.wait_ge(s_oev, NQ)
                if i == 0 and n >= 1:
                    pe.wait_ge(s_yev, n)
                pe.wait_ge(s_hc, u + 2)
                for e in range(2):
                    last = mm(bank(4)[64 * e:64 * e + 64, :], w2s[:, i + e, :], hidc[:, (u + e) % 4, :],
                              start=(i == 0), stop=False, skip_group_check=True)
                if i == 2:
                    t0 = 512 * (n % NCH)
                    for part in range(3):
                        e = part % 2
                        last = mm(bank(4)[64 * e:64 * e + 64, :], wp[0:2 * E, part, 512 + E:],
                                  combT[:, n // NCH % 2, t0:t0 + 512], start=False, stop=(part > 0),
                                  skip_group_check=True)
                last.then_inc(s_dn, 1)

            def result(n):
                pe.wait_ge(s_yev, n + 1)
                if n >= 1:
                    pe.wait_ge(s_z, n)
                for k in range(CH):
                    last = mm(bank(5)[:, 128 * k:128 * k + 128], yT[:, n % 2, 128 * k:128 * k + 128], ident,
                              is_transpose=True, start=True, stop=True)
                last.then_inc(s_y, 1)

            for g in range(NG + 1):
                for s in range(8):
                    u = 8 * g + s
                    if 2 <= u < 8 * NG:
                        up(u)
                    if 1 <= u <= 8 * NG:
                        expand(u - 1)
                    if u >= 4 and u % 2 == 0 and u - 4 < 8 * NG:
                        down(u - 4)
                    if u >= 7 and u % 4 == 3 and (u - 7) // 4 < 2 * NG:
                        result((u - 7) // 4)
                    if s >= 4 and g + 4 < NG:
                        attention_tokens(g + 4, 2 * s - 8, 2 * s - 6)
                    if s == 7 and 0 <= g + 2 < NG:
                        token_transposes(g + 2)
                    if s == 0 and 1 <= g < NG:
                        combine_transposes(g)
                    if s == 1 and g + 1 < NG:
                        router_logits(g + 1)

        @block.scalar
        def _(act):
            a = nc.scalar.activation
            act.dma_start(cst[:, :], consts[:, 0:CONSTS]).then_inc(s_cst, 16)
            act.dma_start(sel_f, consts[0:2 * E, CONSTS:]).then_inc(s_self, 16)

            def h_squares(i):
                act.wait_ge(s_h, i + 1)
                if i >= 2:
                    act.wait_ge(s_ss, i - 1)
                a(squares[:, i % 2], h[:, G * i:G * i + G, :], ACT.Square).then_inc(s_sqf, 1)

            def split_out(i):
                act.wait_ge(s_ftr, 3 * i + 3)
                a(fT[2][:, 1024 * i:1024 * i + 1024], bank(6 + (3 * i + 2) % 2).bitcast(F16),
                  ACT.Copy).then_inc(s_ftev, 1)

            for b in range(B):
                act.wait_ge(s_prod, b + 1)
                a(prod[:, b // 2, 0:NM, b % 2, :], bank(2 * (b % 2), 2).rearrange("p (m v) -> p m v", v=V),
                  ACT.Copy).then_inc(s_prodev, 1)
                if b == 1:
                    act.wait_ge(s_pad, 1)
                    a(prod[:, :, NM, :, :], bank(7).rearrange("p (b c v) -> p b c v", c=2, v=V),
                      ACT.Copy).then_inc(s_padev, 1)
                if b >= 2:
                    h_squares(b - 2)
                if b >= 4:
                    split_out(b - 4)
            h_squares(B - 2)
            split_out(4)
            h_squares(B - 1)

            def sl(n):
                return slice(n * G, n * G + G)

            def attended_squared(x):
                act.wait_ge(s_g, x + 1)
                a(sq_g, f[:, sl(x), :], ACT.Square).then_inc(s_gsq, 1)

            def centred_squared(y):
                act.wait_ge(s_cen, y + 1)
                a(sq_h, h[:, sl(y), :], ACT.Square).then_inc(s_hsq, 1)

            def high_half(y):
                act.wait_ge(s_ln, y + 1)
                a(fs[:, sl(y), 0:D], h[:, sl(y), :], ACT.Copy).then_inc(s_hhi, 1)

            def transposed_out(y):
                act.wait_ge(s_htr, y + 1)
                a(hT[:, 1024 * y:1024 * y + 1024], bank(7).bitcast(F16), ACT.Copy).then_inc(s_htev, 1)

            def combine_out(g):
                act.wait_ge(s_ctr, g + 1)
                if g >= 2:
                    act.wait_ge(s_y, 2 * g - 2)
                a(combT[:, g % 2, :], bank(7).bitcast(F16)[0:2 * E, :], ACT.Copy).then_inc(s_cev, 1)

            def beside(t):
                for i in range(EARLY):
                    at = t - START[i]
                    if at == 25 and i == 0:
                        combine_out(i)
                    if at == 2:
                        attended_squared(i)
                    if at == 8 and i < EARLY - 1:
                        centred_squared(i)
                    if at == 12 and i < EARLY - 1:
                        high_half(i)
                    if at == 15 and i < EARLY - 1:
                        transposed_out(i)

            def exps(q, first, last=False):
                for k in range(NT):
                    if first and k % 2 == 0 and k // 2 - 1 in LATE_SPLITS:
                        split_out(LATE_SPLITS[k // 2 - 1])
                    act.wait_ge(s_sc, q * NT + k + 1)
                    if not (first and k < 4):
                        act.wait_ge(s_pv, q * PAIRS + k // 2 - 1)
                    a(probs[:, k % 4, :], bank(2 * (k % 2), 2), ACT.Exp,
                      accum_out=rowsum[:, bass.ds(q * NT + k, 1)]).then_inc(s_pr, 1)
                    if last and k % 2:
                        beside(k // 2)
            exps(0, True)
            with act.Fori(1, NQ - 1) as q:
                exps(q, False)
            exps(NQ - 1, False, True)

            act.wait_ge(s_w1r, 64)
            act.wait_ge(s_pv, NQ * PAIRS - 1)
            for g in range(NG + 2):
                for s in range(8):
                    u, x, y, z = 8 * g + s, g + 3, g + 2, g - 1
                    if u < 8 * NG:
                        act.wait_ge(s_up, u + 1)
                        if u >= 4:
                            act.wait_ge(s_hc, u - 3)
                        a(hid[:, u % 4, :], bank(u % 2), ACT.Gelu, bias=b1s[:, u % 4:u % 4 + 1]).then_inc(s_gelu, 1)
                    if s == 0 and 1 <= g < NG:
                        combine_out(g)
                    if u >= 6 and u % 4 == 2 and (u - 6) // 4 < 2 * NG:
                        n = (u - 6) // 4
                        act.wait_ge(s_dn, 2 * n + 2)
                        if n >= 2:
                            act.wait_ge(s_y, n - 1)
                        a(yT[:, n % 2, :], bank(4), ACT.Copy).then_inc(s_yev, 1)
                    if s == 1 and x < NG:
                        attended_squared(x)
                    if s == 1 and y < NG:
                        centred_squared(y)
                    if s == 5 and y < NG:
                        high_half(y)
                    if s == 7 and y < NG:
                        transposed_out(y)
                    if s == 0 and 0 <= z - 1 < NG:
                        act.wait_ge(s_cen2, z)
                        a(sq_o, h[:, sl(z - 1), :], ACT.Square).then_inc(s_osq, 1)

        @block.vector
        def _(dve):
            tt, ts, cp, red = nc.vector.tensor_tensor, nc.vector.tensor_scalar, nc.vector.tensor_copy, nc.vector.tensor_reduce
            stt = nc.vector.scalar_tensor_tensor

            def wide(v, n, d=D):
                return v.unsqueeze(2).to_broadcast([128, n, d])

            dve.wait_ge(s_wfold, 1)
            raw = ps[:, 0:NF * D].rearrange("p (g o) -> p g o", o=D)
            for s in range(HALF):
                tt(wdft[s], raw, wide(dft[:, s, :], NF), ALU.mult).then_inc(s_fold, 1)
            for s in range(HALF):
                dve.wait_ge(s_fold, s + 1)
                by_f = wdft[s].rearrange("p (r f) o -> p o r f", r=2)
                for odd in range(2):
                    last = red(wpar[:, odd, s, :], by_f[:, :, :, odd::2], AX.XY, ALU.add)
            last.then_inc(s_fold, 1)
            dve.wait_ge(s_fold, HALF + 1)
            tt(weff[:, :, 0:D], wpar[:, 0], wpar[:, 1], ALU.add)
            tt(weff[:, :, D:2 * D], wpar[:, 0], wpar[:, 1], ALU.subtract).then_inc(s_weff, 1)
            dve.wait_ge(s_weff, 1)
            red(wpad[:, :], weff[:, :, :].rearrange("p s k -> p k s"), AX.X, ALU.add).then_inc(s_wpad, 1)
            then = chained(dve, s_ch[0])

            def tokens_out(i):
                dve.wait_ge(s_tr, i + 1)
                red(h[:, 8 * i:8 * i + 8, :], bank(4, 2).rearrange("p (s n o) -> p n o s", s=2, o=D),
                    AX.X, ALU.add).then_inc(s_h, 1)

            def norms(i):
                sl = slice(G * i, G * i + G)
                dve.wait_ge(s_sqf, i + 1)
                then(red(stat[:, 0, sl], squares[:, i % 2], AX.X, ALU.add))
                ts(stat[:, 1, sl], stat[:, 0, sl], 1e-24, None, ALU.max).then_inc(s_ss, 1)

            def normed(i):
                sl = slice(G * i, G * i + G)
                dve.wait_ge(s_rt, i + 1)
                then(tt(f[:, sl, :], h[:, sl, :], wide(stat[:, 2, sl], G), ALU.mult))
                then(cp(fs[:, sl, 0:D], f[:, sl, :]))
                tt(fs[:, sl, D:2 * D], f[:, sl, :], fs[:, sl, 0:D], ALU.subtract).then_inc(s_fs, 1)

            def splits_out(i):
                for kind in range(2):
                    n = 3 * i + kind
                    dve.wait_ge(s_ftr, n + 1)
                    cp(fT[kind][:, 1024 * i:1024 * i + 1024], bank(6 + n % 2).bitcast(F16)).then_inc(s_ftev2, 1)

            for b in range(2, B):
                tokens_out(b - 2)
                if b >= 4:
                    splits_out(b - 4)
                norms(b - 2)
                normed(b - 2)
            tokens_out(B - 2)
            splits_out(4)
            norms(B - 2)
            tokens_out(B - 1)
            normed(B - 2)
            norms(B - 1)
            normed(B - 1)

            def low_parts(q, first, last=False):
                for k in range(NT):
                    if first and k % 2 == 0 and k // 2 - 1 in LATE_SPLITS:
                        splits_out(LATE_SPLITS[k // 2 - 1])
                    dve.wait_ge(s_pr, q * NT + k + 1)
                    if not (first and k < 4):
                        dve.wait_ge(s_pv, q * PAIRS + k // 2 - 1)
                    tt(probs_lo[:, k % 4, :], probs[:, k % 4, :], probs[:, k % 4, :].bitcast(BF16)[:, 1:2 * QC:2],
                       ALU.subtract).then_inc(s_lo, 1)
                    if k == 0 and not first:
                        sums_out(q - 1)
                    if last and k % 2:
                        beside(k // 2)

            def sums_out(q):
                dve.wait_ge(s_pv, (q + 1) * PAIRS)
                cp(outT[:, bass.ds(q * QC, QC)], bank(4, 2)).then_inc(s_oev, 1)

            then = chained(dve, s_ch[1])

            def shares(n0, n1):
                t = slice(n0 * G, n1 * G)
                then(red(stat[:, 4, t], rowsum[:, :].rearrange("p (q k) -> p k q", q=NQ)[:, t, :], AX.X, ALU.add))
                then(nc.vector.reciprocal(stat[:, 5, t], stat[:, 4, t]))
                then(ts(stat[:, 6, t], stat[:, 5, t], 1.0 - 0.8, None, ALU.mult))

            def sl(n):
                return slice(n * G, n * G + G)

            def attended(x):
                dve.wait_ge(s_at, x + 1)
                tt(att, bank(6).rearrange("p (j o) -> p j o", o=D), wide(stat[:, 6, sl(x)], G),
                   ALU.mult).then_inc(s_att, 1)
                dve.wait_ge(s_att, x + 1)
                stt(f[:, sl(x), :], f[:, sl(x), :], 0.8, att, ALU.mult, ALU.add).then_inc(s_g, 1)

            def attended_squares(x):
                dve.wait_ge(s_gsq, x + 1)
                then(red(stat[:, 5, sl(x)], sq_g, AX.X, ALU.add))
                ts(stat[:, 0, sl(x)], stat[:, 5, sl(x)], 1e-24, None, ALU.max).then_inc(s_ss1, 1)

            def attended_normed(x):
                dve.wait_ge(s_rn, x + 1)
                tt(f[:, sl(x), :], f[:, sl(x), :], wide(stat[:, 1, sl(x)], G), ALU.mult).then_inc(s_gn, 1)

            def mean(n, ready, done):
                dve.wait_ge(*ready)
                then(red(stat[:, 5, sl(n)], h[:, sl(n), :], AX.X, ALU.add))
                ts(stat[:, 2, sl(n)], stat[:, 5, sl(n)], 1.0 / D, None, ALU.mult).then_inc(done, 1)

            def variance(n, squares, ready, done):
                dve.wait_ge(*ready)
                then(red(stat[:, 5, sl(n)], squares, AX.X, ALU.add))
                ts(stat[:, 3, sl(n)], stat[:, 5, sl(n)], 1.0 / D, 1e-5, ALU.mult, ALU.add).then_inc(done, 1)

            def scaled(n, ready, done):
                dve.wait_ge(*ready)
                tt(h[:, sl(n), :], h[:, sl(n), :], wide(stat[:, 7, sl(n)], G), ALU.mult).then_inc(done, 1)

            def by_tile(v):
                return v.rearrange("p (t e) -> p t e", e=E)

            def R(i):
                return by_tile(rtmp[:, i, :])

            def of_tile(i):
                return wide(rsmall[:, i, :], G, E)

            numbers = enum.unsqueeze(1).to_broadcast([128, G, E])
            STEPS = 14
            ORDER = (0, 1, 2, 3, 4, 5, 6, 8, 7, 9, 10, 11, 12, 13)
            NEEDS = {1: 0, 2: 1, 3: 2, 4: 3, 5: 4, 6: 5, 7: 6, 9: 8, 10: 7, 11: 10, 12: 11, 13: 12, 14: 13}

            def logits_out(y):
                dve.wait_ge(s_lg, y + 1)
                logits = by_tile(bank(7)[:, 0:G * E])
                then(red(rsmall[:, 0, :], logits, AX.X, ALU.max))
                tt(R(0), logits, of_tile(0), ALU.subtract).then_inc(s_centred, 1)

            def route(y, step):
                if step in NEEDS:
                    dve.wait_ge(s_route, STEPS * y + ORDER.index(NEEDS[step]) + 1)
                else:
                    dve.wait_ge(s_centred, y + 1)
                if step == 0:
                    stt(R(2), R(0), 0.0, numbers, ALU.is_equal, ALU.mult).then_inc(s_route, 1)
                if step == 1:
                    red(rsmall[:, 1, :], R(2), AX.X, ALU.min).then_inc(s_route, 1)
                if step == 2:
                    tt(R(3), numbers, of_tile(1), ALU.is_equal).then_inc(s_route, 1)
                if step == 3:
                    stt(R(4), R(3), -1e30, R(0), ALU.mult, ALU.add).then_inc(s_route, 1)
                if step == 4:
                    red(rsmall[:, 2, :], R(4), AX.X, ALU.max).then_inc(s_gap, 1)
                    dve.wait_ge(s_gap, y + 1)
                    tt(R(5), R(4), of_tile(2), ALU.is_equal).then_inc(s_route, 1)
                if step == 5:
                    tt(R(6), R(5), numbers, ALU.mult).then_inc(s_route, 1)
                if step == 6:
                    red(rsmall[:, 4, :], R(6), AX.X, ALU.min).then_inc(s_route, 1)
                if step == 7:
                    tt(R(7), numbers, of_tile(4), ALU.is_equal).then_inc(s_route, 1)
                if step == 8:
                    dve.wait_ge(s_exp, y + 1)
                    ts(rsmall[:, 5, :], rsmall[:, 3, :], 1.0, None, ALU.add).then_inc(s_route, 1)
                if step == 9:
                    nc.vector.reciprocal(rsmall[:, 6, :], rsmall[:, 5, :]).then_inc(s_route, 1)
                if step == 10:
                    tt(R(8), R(7), of_tile(3), ALU.mult).then_inc(s_route, 1)
                if step == 11:
                    tt(R(9), R(8), R(3), ALU.add).then_inc(s_route, 1)
                if step == 12:
                    tt(R(10), R(9), of_tile(6), ALU.mult).then_inc(s_route, 1)
                if step == 13:
                    if y >= 2:
                        dve.wait_ge(s_ctr, y - 1)
                    cp(combine[:, y % 2, :, 0:E], R(10)).then_inc(s_route, 1)
                if step == 14:
                    tt(combine[:, y % 2, :, E:2 * E], R(10), combine[:, y % 2, :, 0:E], ALU.subtract).then_inc(s_comb, 1)

            def weigh(u):
                dve.wait_ge(s_gelu, u + 1)
                dve.wait_ge(s_ex, u + 1)
                if u >= 4:
                    dve.wait_ge(s_dn, u // 2 - 1)
                tt(hidc[:, u % 4, :], hid[:, u % 4, :], bank(2 + u % 2), ALU.mult).then_inc(s_hc, 1)

            def residual(n):
                dve.wait_ge(s_y, n + 1)
                t = slice(CH * n, CH * n + CH)
                y = bank(5).rearrange("p (j s o) -> p j s o", s=2, o=D)
                then(stt(h[:, t, :], h[:, t, :], 2.0, y[:, :, 0, :], ALU.mult, ALU.add))
                tt(h[:, t, :], h[:, t, :], y[:, :, 1, :], ALU.add).then_inc(s_z, 1)

            STEPS_OF = {1: ((), (), (0,)), 2: ((), (1,), (2,)), 3: ((), (3,), ()), 4: ((), (4,), (5,)),
                        5: ((), (6,), (8, 7)), 6: ((9, 10), (11,), ()), 7: ((), (12,), (13,))}
            def beside(t):
                for i in range(EARLY):
                    at = t - START[i]
                    if at == 0:
                        shares(i, i + 1)
                        attended(i)
                    if at == 13 and i == EARLY - 1:
                        shares(EARLY, EARLY + 1)
                        attended(EARLY)
                    if at == 3:
                        attended_squares(i)
                    if at == 6:
                        mean(i, (s_res, i + 1), s_mean)
                    if at == 9 and i < EARLY - 1:
                        variance(i, sq_h, (s_hsq, i + 1), s_var)
                    if at >= 17 and i == 0:
                        if at == 17:
                            logits_out(i)
                        for step in (ORDER + (STEPS,))[max(0, 3 * (at - 18)):max(0, 3 * (at - 18) + 3)]:
                            route(i, step)

            low_parts(0, True)
            with dve.Fori(1, NQ - 1) as q:
                low_parts(q, False)
            dve.wait_ge(s_wp, 1)
            low_parts(NQ - 1, False, True)
            sums_out(NQ - 1)
            for g in range(NG + 3):
                for s in range(8):
                    u, x, y, q, z = 8 * g + s, g + 3, g + 2, g + 1, g - 1
                    steps = STEPS_OF.get(s, ((),) * 3) if 0 <= q < NG else ((),) * 3
                    for step in steps[0]:
                        route(q, step)
                    if 1 <= u <= 8 * NG:
                        weigh(u - 1)
                    if s == 1 and 0 <= q < NG:
                        logits_out(q)
                    if s == 0 and 1 <= g < NG:
                        route(g, STEPS)
                    for step in steps[1]:
                        route(q, step)
                    if u >= 8 and u % 4 == 0 and (u - 8) // 4 < 2 * NG:
                        residual((u - 8) // 4)
                    if s == 0 and EARLY < x < NG:
                        attended(x)
                    if s == 3 and x == EARLY:
                        shares(EARLY + 1, NG)
                    if s == 0 and 1 <= z <= NG:
                        variance(z - 1, sq_o, (s_osq, z), s_var2)
                    if s == 2 and x < NG:
                        attended_squares(x)
                    if s == 2 and 0 <= y < NG:
                        variance(y, sq_h, (s_hsq, y + 1), s_var)
                    if s == 4 and x < NG:
                        attended_normed(x)
                    if s == 4 and 0 <= y < NG:
                        scaled(y, (s_rstd, y + 1), s_ln)
                    if s == 7 and x < NG:
                        mean(x, (s_res, x + 1), s_mean)
                    if s == 5 and 0 <= z < NG:
                        mean(z, (s_z, 2 * z + 2), s_mean2)
                    for step in steps[2]:
                        route(q, step)


_INS = ["x", "L0_tok_W", "L0_ffn_router_w", "L0_ffn_w1", "L0_ffn_b1", "L0_ffn_w2", "L0_ffn_b2"]


def kernel(**inputs):
    import numpy as _np
    import concourse.bacc as _bacc
    from concourse import mybir as _mybir
    from concourse.bass_utils import run_bass_kernel_spmd as _run

    nc = _bacc.Bacc("TRN2", target_bir_lowering=False, num_devices=1)
    arrays, args = {}, []
    for name in _INS:
        a = _np.ascontiguousarray(inputs[name])
        arrays[f"in_{name}_dram"] = a
        args.append(nc.dram_tensor(f"in_{name}_dram", a.shape, _mybir.dt.from_np(a.dtype), kind="ExternalInput").ap())
    c = constants()
    arrays["consts_dram"] = c
    args.append(nc.dram_tensor("consts_dram", c.shape, _mybir.dt.from_np(c.dtype), kind="ExternalInput").ap())
    args.append(nc.dram_tensor("out_dram", (B, V * NP, D), _mybir.dt.float32, kind="ExternalOutput").ap())
    tower(nc, *args)
    r = _run(nc, [arrays], core_ids=[0])
    return r.results[0]["out_dram"]
```
